# Optimizing a Trainium2 kernel written in Bass

```python
import numpy as np
import jax
import jax.numpy as jnp

def _softmax(x, axis=-1):
    return jax.nn.softmax(x, axis=axis)

def _gelu(x):
    return jax.nn.gelu(x, approximate=True)

def _silu(x):
    return jax.nn.silu(x)

def _sigmoid(x):
    return jax.nn.sigmoid(x)

def _layernorm(x, axis=-1, eps=1e-05):
    m = jnp.mean(x, axis=axis, keepdims=True)
    v = jnp.var(x, axis=axis, keepdims=True)
    return (x - m) / jnp.sqrt(v + eps)

def _scatter_add(tgt, idx, src, axis=0):
    return tgt.at[idx].add(src)

def _segment_sum(src, seg, n):
    return jax.ops.segment_sum(src, seg, n)
kernel_name = 'mk_xattn_seq_d1_seqx_r4_e59146'

def setup_inputs(seed: int=0):
    np.random.seed(seed)
    _w = jnp.asarray

    def _rec_inputs():
        import jax
        import jax.numpy as jnp
        _rk = jax.random.key(seed)
        x = -0.0002928 + 1 * jax.random.normal(jax.random.fold_in(_rk, 1), (8, 512, 256), jnp.float32)
        _lenS = 512 - jax.random.randint(jax.random.fold_in(_rk, 7), (8,), 0, max(1, 512 // 4) + 1, jnp.int32)
        _lenS2 = 1601 - jax.random.randint(jax.random.fold_in(_rk, 8), (8,), 0, max(1, 1601 // 4) + 1, jnp.int32)
        _ctx_1024P = jax.random.normal(jax.random.fold_in(_rk, 11), (8, 16, 256), jnp.float32)
        _ctx_1024c = jax.random.dirichlet(jax.random.fold_in(_rk, 511), 0.3 * jnp.ones((16,), jnp.float32), (8, 1601))
        _ctx_1024t = jnp.einsum('bsk,bkd->bsd', _ctx_1024c, _ctx_1024P)
        _ctx_1024t = _ctx_1024t * jax.lax.rsqrt(jnp.mean(jnp.square(_ctx_1024t)) + 1e-12) * 0.953939
        ctx_1024 = 4.13588e-05 + 0.999923 * (_ctx_1024t + 0.3 * jax.random.normal(jax.random.fold_in(_rk, 611), (8, 1601, 256), jnp.float32))
        return (x, ctx_1024)
    x, ctx_1024 = _rec_inputs()

    def _L0_xattn_setup():
        import jax, jax.numpy as jnp
        import numpy as np
        N_HEAD = 16
        Q_DIM = 256
        V_DIM = 256
        LN_EPS = 1e-05
        key = jax.random.key(seed)
        ks = jax.random.split(key, 13)
        b, lq, lv = (4, 256, 512)
        s_q = 1.0 / np.sqrt(Q_DIM)
        s_v = 1.0 / np.sqrt(V_DIM)
        return {'q': jax.random.normal(ks[0], (b, lq, Q_DIM), jnp.float32), 'k': jax.random.normal(ks[1], (b, lv, Q_DIM), jnp.float32), 'v': jax.random.normal(ks[2], (b, lv, V_DIM), jnp.float32), 'Wq': jax.random.normal(ks[3], (Q_DIM, Q_DIM), jnp.float32) * s_q, 'bq': jnp.zeros((Q_DIM,), jnp.float32), 'Wk': jax.random.normal(ks[4], (Q_DIM, Q_DIM), jnp.float32) * s_q, 'bk': jnp.zeros((Q_DIM,), jnp.float32), 'Wv': jax.random.normal(ks[5], (V_DIM, V_DIM), jnp.float32) * s_v, 'bv': jnp.zeros((V_DIM,), jnp.float32), 'Wo': jax.random.normal(ks[6], (V_DIM, V_DIM), jnp.float32) * s_v, 'bo': jnp.zeros((V_DIM,), jnp.float32), 'ln_g': jnp.ones((V_DIM,), jnp.float32), 'ln_b': jnp.zeros((V_DIM,), jnp.float32)}
    _L0_xattn_all = _L0_xattn_setup()
    _L0_xattn_in = {k: v for k, v in _L0_xattn_all.items() if k in ('Wq', 'bq', 'Wk', 'bk', 'Wv', 'bv', 'Wo', 'bo', 'ln_g', 'ln_b')}
    del _L0_xattn_all
    return {'x': x, 'ctx_1024': ctx_1024, 'L0_xattn_Wq': _L0_xattn_in['Wq'], 'L0_xattn_bq': _L0_xattn_in['bq'], 'L0_xattn_Wk': _L0_xattn_in['Wk'], 'L0_xattn_bk': _L0_xattn_in['bk'], 'L0_xattn_Wv': _L0_xattn_in['Wv'], 'L0_xattn_bv': _L0_xattn_in['bv'], 'L0_xattn_Wo': _L0_xattn_in['Wo'], 'L0_xattn_bo': _L0_xattn_in['bo'], 'L0_xattn_ln_g': _L0_xattn_in['ln_g'], 'L0_xattn_ln_b': _L0_xattn_in['ln_b']}

def reference(x, ctx_1024, L0_xattn_Wq, L0_xattn_bq, L0_xattn_Wk, L0_xattn_bk, L0_xattn_Wv, L0_xattn_bv, L0_xattn_Wo, L0_xattn_bo, L0_xattn_ln_g, L0_xattn_ln_b):
    import jax
    import jax.numpy as jnp

    def _L0_xattn_ref(q, k, v, Wq, bq, Wk, bk, Wv, bv, Wo, bo, ln_g, ln_b):
        import jax, jax.numpy as jnp
        import numpy as np
        N_HEAD = 16
        Q_DIM = 256
        V_DIM = 256
        LN_EPS = 1e-05
        b, lq, _ = q.shape
        lv = k.shape[1]
        qh = Q_DIM // N_HEAD
        vh = V_DIM // N_HEAD
        q_ = (q @ Wq + bq).reshape(b, lq, N_HEAD, qh)
        k_ = (k @ Wk + bk).reshape(b, lv, N_HEAD, qh)
        v_ = (v @ Wv + bv).reshape(b, lv, N_HEAD, vh)
        scores = jnp.einsum('bqhd,bkhd->bhqk', q_, k_) / np.sqrt(qh).astype(jnp.float32)
        attn = jax.nn.softmax(scores, axis=-1)
        out = jnp.einsum('bhqk,bkhd->bqhd', attn, v_).reshape(b, lq, V_DIM)
        out = out @ Wo + bo
        resid = q[..., :V_DIM] if V_DIM < Q_DIM else q
        x = resid + out
        mu = jnp.mean(x, axis=-1, keepdims=True)
        var = jnp.mean(jnp.square(x - mu), axis=-1, keepdims=True)
        return (x - mu) / jnp.sqrt(var + LN_EPS) * ln_g + ln_b
    x = _L0_xattn_ref(x, ctx_1024, ctx_1024, L0_xattn_Wq, L0_xattn_bq, L0_xattn_Wk, L0_xattn_bk, L0_xattn_Wv, L0_xattn_bv, L0_xattn_Wo, L0_xattn_bo, L0_xattn_ln_g, L0_xattn_ln_b)
    return x

_drawn_inputs = setup_inputs


def setup_inputs(seed=0):
    import zlib

    import numpy as np

    out = dict(_drawn_inputs(seed))
    spreads = {'L0_xattn_bq': (0.0, 0.401),
     'L0_xattn_bk': (0.0, 0.8),
     'L0_xattn_bv': (0.0, 0.1),
     'L0_xattn_bo': (0.0, 0.1),
     'L0_xattn_ln_g': (1.0, 0.2),
     'L0_xattn_ln_b': (0.0, 0.1)}
    factors = {}
    for name, (base, spread) in spreads.items():
        noise = np.random.default_rng([zlib.crc32(name.encode()), seed]).standard_normal(out[name].shape)
        drawn = base * np.exp(spread * noise) if base else spread * noise
        out[name] = jnp.asarray(drawn.astype(out[name].dtype))
    for name, factor in factors.items():
        out[name] = (out[name] * factor).astype(out[name].dtype)
    return out
```

```python
from contextlib import ExitStack

import concourse.bass as bass
from concourse import mybir

F32 = mybir.dt.float32
BF16 = mybir.dt.bfloat16
ALU = mybir.AluOpType
ACT = mybir.ActivationFunctionType
AX = mybir.AxisListType

P = 128
BANK = 512
BATCHES, QUERIES, DIM = 8, 512, 256
KEYS = 1601
HEADS, HD = 16, 16
LN_EPS = 1e-5

HALVES = DIM // P
GROUP = 4
GROUPS = HEADS // GROUP
UNITS = BATCHES * GROUPS
QTILES = QUERIES // P
FULL = KEYS // P
REST = KEYS - FULL * P
KTILES = FULL + 1
CHUNKS = [BANK] * (KEYS // BANK) + [KEYS % BANK]
assert CHUNKS[-1] == REST and QUERIES == BANK
PARTS = 3
PROD = 6 * HD
ROWS = PROD + PARTS
KPITCH = KEYS + 7
VW = HD + 1
SCALE = 1.0 / HD ** 0.5

PIECES = ([("xt", h, 0) for h in range(HALVES)]
          + [("ct", h, c) for c in range(len(CHUNKS)) for h in range(HALVES)]
          + [("v", t, 0) for t in range(0, KTILES, 2)]
          + [("k", m, c) for m in range(HALVES) for c in range(len(CHUNKS))]
          + [("q", m, 0) for m in range(HALVES)])
NPIECES = len(PIECES)
TURNS = sum(p[0] in ("xt", "ct") for p in PIECES)
BY_DVE = [p[0] == "v" for p in PIECES]
ACT_PIECES, DVE_PIECES = NPIECES - sum(BY_DVE), sum(BY_DVE)
BANKS = 8
SPLITS = 4

RING = 3
SMAX = QTILES * (len(CHUNKS) - 1) + 1
PERIOD = GROUP * SMAX + 1
LEAD = 12
TURN_AT = 2
PBUFS = 4
SHIFT_STEPS = 5


def period(r):
    items = [("s", r, h, j) for h in range(GROUP) for j in range(SMAX)]
    return items[:TURN_AT] + [("m", r - 1)] + items[TURN_AT:]


ENDING = ([(4 + t, ("o", t)) for t in range(QTILES)]
          + [(8 + t, ("n", t // 2)) for t in range(0, QTILES, 2)]
          + [(12 + 2 * t, ("y", t)) for t in range(QTILES)])
LOOP_ITEMS = GROUPS * PERIOD + len(ENDING)
assert LOOP_ITEMS % RING == 0 and (GROUPS * KTILES) % PBUFS == 0


def spread(items, ending):
    slots = [[] for _ in range(2 * KTILES)]
    for n, it in enumerate(items):
        slots[n * 2 * KTILES // len(items)].append(it)
    for half, it in ending:
        slots[half].insert(0, it)
    return slots


def is_first(b):
    return isinstance(b, int) and b == 0


class Plan:

    def __init__(self):
        first = [it for it in period(0) if it[0] == "s"] + period(1)[:LEAD]
        self.count = 0
        self.prologue = self.numbered([first])[0]
        self.unit0 = self.unit(0, [])
        self.loop_start = self.count
        self.body = [self.unit(r, ENDING if r == GROUPS else []) for r in range(1, GROUPS + 1)]
        assert self.count == self.loop_start + LOOP_ITEMS
        self.count = self.loop_start
        self.tail = [self.unit(1, []), self.unit(2, [], last=True), self.unit(3, [], none=True)]
        self.ending = self.numbered([[it for _, it in ENDING]])[0]
        self.turn_of = {}
        for b, units in ((0, [[self.prologue], self.unit0]), (None, self.body), (BATCHES - 1, self.tail)):
            self.turn_of |= {(b, it[1]): n for slots in units for slot in slots for n, it in slot if it[0] == "m"}
        at = {it: n for slots in self.body for slot in slots for n, it in slot}
        self.turned = at[("o", QTILES - 1)] - LOOP_ITEMS

    def numbered(self, slots):
        out = []
        for slot in slots:
            out.append([(self.count + n, it) for n, it in enumerate(slot)])
            self.count += len(slot)
        return out

    def unit(self, r, ending, last=False, none=False):
        items = period(r + 1)[LEAD:] + period(r + 2)[:LEAD]
        if last:
            items = period(r + 1)[LEAD:] + [("m", r + 1)]
        return self.numbered(spread([] if none else items, ending))


def xattn_kernel(nc, x, ctx, Wq, bq, Wk, bk, Wv, bv, Wo, bo, ln_g, ln_b, out):
    plan = Plan()
    kparts = nc.dram_tensor("kparts", [BATCHES, HEADS, PARTS * HD, KEYS], BF16, kind="Internal").ap()
    qparts = nc.dram_tensor("qparts", [BATCHES, HEADS, PARTS * HD, QUERIES], BF16, kind="Internal").ap()
    vunits = nc.dram_tensor("vunits", [BATCHES, GROUPS, P, KTILES * GROUP * VW], F32, kind="Internal").ap()

    with ExitStack() as stack:
        def sb(name, shape, dt):
            return stack.enter_context(nc.sbuf_tensor(name, shape, dt))

        def sem(name):
            return stack.enter_context(nc.semaphore(name))

        ident = sb("ident", [P, P], F32)
        identb = sb("identb", [P, P], BF16)
        zeros = sb("zeros", [P, BANK], BF16)
        wq, wk, wv, wo = (sb(n, [P, HALVES, DIM], F32) for n in ("wq", "wk", "wv", "wo"))
        bq_col, bk_col = (sb(n, [P, HALVES], F32) for n in ("bq_col", "bk_col"))
        bv_row, bo_row, g_row, b_row = (sb(n, [P, DIM], F32) for n in ("bv_row", "bo_row", "g_row", "b_row"))
        minus_half = sb("minus_half", [P, 1], F32)
        eps = sb("eps", [P, 1], F32)
        probs = sb("probs", [P, PBUFS, GROUP * BANK], F32)
        flat = probs[:, :, :].rearrange("p a b -> p (a b)")
        ctx_in = flat[:, 0:KTILES * DIM].rearrange("p (t d) -> p t d", t=KTILES)
        ctxT = flat[:, KTILES * DIM:KTILES * DIM + HALVES * KEYS].rearrange("p (h k) -> p h k", h=HALVES)
        x_in = sb("x_in", [P, QTILES, DIM], F32)
        xT = sb("xT", [P, HALVES, QUERIES], F32)
        kf = sb("kf", [P, HALVES, KEYS], F32)
        qf = sb("qf", [P, HALVES, QUERIES], F32)
        left = sb("left", [P, KEYS], F32)
        kp = sb("kp", [P, HALVES, PARTS, KEYS], BF16)
        qp = sb("qp", [P, HALVES, PARTS, QUERIES], BF16)
        v_out = sb("v_out", [P, GROUPS, KTILES, GROUP, VW], F32)
        keys = [sb(f"keys{g}", [ROWS, GROUP, KPITCH], BF16) for g in range(GROUPS)]
        qrys = [sb(f"qrys{g}", [ROWS, GROUP, QUERIES], BF16) for g in range(GROUPS)]
        vals = [sb(f"vals{g}", [P, KTILES, GROUP, VW], F32) for g in range(GROUPS)]
        mx = [sb(f"mx{n}", [P, GROUP, QTILES, len(CHUNKS)], F32) for n in range(2)]
        neg = [sb(f"neg{n}", [P, GROUP * QTILES], F32) for n in range(2)]
        negleft = [sb(f"negleft{n}", [P, GROUP * QTILES], F32) for n in range(2)]
        negpad = [sb(f"negpad{n}", [P, P], BF16) for n in range(2)]
        negparts = [t[:, 0:PARTS * GROUP * QTILES].rearrange("p (i n) -> p i n", i=PARTS) for t in negpad]
        negT = [sb(f"negT{n}", [PARTS * GROUP * QTILES, P], BF16) for n in range(2)]
        def over(tensor, start, *dims):
            n = 1
            for d in dims:
                n *= d
            names = "abc"[:len(dims)]
            return tensor[:, start:start + n].rearrange(
                f"p ({' '.join(names)}) -> p {' '.join(names)}", **dict(zip(names, dims)))

        kf_flat = kf[:, :, :].rearrange("p h k -> p (h k)")
        o_out = over(v_out[:, :, :, :, :].rearrange("p g t h w -> p (g t h w)"), 0, GROUPS, QUERIES)
        rden = sb("rden", [P, QTILES, HEADS], F32)
        o_norm = over(kf_flat, 0, QTILES, HEADS, HD)
        o_normT = over(kf_flat, QTILES * DIM, QTILES, HALVES, P)
        resid = sb("resid", [P, QTILES, DIM], F32)
        y = over(kf_flat, 2 * QTILES * DIM, QTILES, DIM)
        stats = sb("stats", [P, QTILES, 6], F32)
        mv = sb("mv", [P, QTILES, 2], F32)
        rstd = sb("rstd", [P, QTILES, 2], F32)
        z = over(left, 0, QTILES, DIM)

        psum = stack.enter_context(nc.psum_tensor("psum", [P, BANKS, BANK], F32))
        s_bank = [[psum[:, 2 * p + n, :] for n in range(2)] for p in range(2)]
        s_pair = [psum[:, 2 * p:2 * p + 2, :].rearrange("p a b -> p (a b)") for p in range(2)]
        ring = [psum[:, 4 + n, :] for n in range(RING)]
        o_bank = psum[:, BANKS - 1, :]

        weights_loaded = sem("weights_loaded")
        rows_loaded = sem("rows_loaded")
        ident_cleared = sem("ident_cleared")
        ident_made = sem("ident_made")
        consts_made = sem("consts_made")
        ones_made = sem("ones_made")
        x_loaded = sem("x_loaded")
        ctx_loaded = sem("ctx_loaded")
        piece_made = sem("piece_made")
        act_took = sem("act_took")
        dve_took = sem("dve_took")
        split_step = sem("split_step")
        v_written = sem("v_written")
        kq_written = sem("kq_written")
        kq_loaded = [sem(f"kq_loaded{g}") for g in range(GROUPS)]
        v_loaded = [sem(f"v_loaded{g}") for g in range(GROUPS)]
        item_made = sem("item_made")
        item_taken = sem("item_taken")
        shift_step = sem("shift_step")
        shift_placed = [sem(f"shift_placed{g}") for g in range(GROUPS)]
        scores_ready = sem("scores_ready")
        probs_ready = sem("probs_ready")
        pv_done = sem("pv_done")
        o_copied = sem("o_copied")
        rden_ready = sem("rden_ready")
        y_ready = sem("y_ready")
        stats_ready = sem("stats_ready")
        mv_ready = sem("mv_ready")
        resid_loaded = sem("resid_loaded")
        resid_ready = sem("resid_ready")
        norm_step = sem("norm_step")
        out_written = sem("out_written")
        KQ_DMAS, V_DMAS = 9, 1
        KQ_WRITES = 2 * HALVES * PARTS
        WEIGHTS, ROWS_N = 6, 4
        NORM_STEPS = 6
        CONSTS = 2 + 2 + 1

        def vitem(b, r):
            return b + r // GROUPS, r % GROUPS

        block = stack.enter_context(nc.Block())

        @block.sync
        def _(sp):
            for t, w in ((wq, Wq), (wk, Wk), (wv, Wv), (wo, Wo)):
                sp.dma_start(t[:, :, :], w.rearrange("(h p) n -> p h n", p=P)).then_inc(weights_loaded, 16)
            with nc.allow_non_contiguous_dma("two columns of biases"):
                for t, v in ((bq_col, bq), (bk_col, bk)):
                    sp.dma_start(t[:, :], v.rearrange("(h p) -> p h", p=P)).then_inc(weights_loaded, 16)

            def load_inputs(b):
                sp.dma_start(x_in[:, :, :], x[b].rearrange("(t p) d -> p t d", p=P)).then_inc(x_loaded, 16)
                sp.dma_start(ctx_in[:, 0:FULL, :],
                             ctx[b, 0:FULL * P, :].rearrange("(t p) d -> p t d", p=P)).then_inc(ctx_loaded, 16)
                sp.dma_start(ctx_in[0:REST, FULL, :], ctx[b, FULL * P:KEYS, :]).then_inc(ctx_loaded, 16)

            def store_parts(b):
                sp.wait_ge(dve_took, DVE_PIECES * (b + 1))
                sp.dma_start(vunits[b].rearrange("g p n -> p g n"),
                             v_out[:, :, :, :, :].rearrange("p g t h w -> p g (t h w)")).then_inc(v_written, 16)
                for n, (src, dst) in enumerate(((kp, kparts), (qp, qparts))):
                    for m in range(HALVES):
                        sp.wait_ge(split_step, 2 * HALVES * SPLITS * b + (n * HALVES + m + 1) * SPLITS)
                        for i in range(PARTS):
                            sp.dma_start(
                                dst[b, m * HEADS // HALVES:(m + 1) * HEADS // HALVES, i * HD:(i + 1) * HD, :],
                                src[:, m, i, :]).then_inc(kq_written, 16)

            load_inputs(0)
            with sp.Fori(0, BATCHES - 1) as b:
                sp.wait_ge(piece_made, NPIECES * b + TURNS)
                load_inputs(b + 1)
                store_parts(b)
            store_parts(BATCHES - 1)

            def load_unit(b, g):
                heads = slice(g * GROUP, (g + 1) * GROUP)
                row = 0
                for n in (3, 2, 1):
                    sp.dma_start(keys[g][row:row + n * HD, :, 0:KEYS],
                                 kparts[b, heads, 0:n * HD, :].rearrange("h r k -> r h k")
                                 ).then_inc(kq_loaded[g], 16)
                    for _ in range(n):
                        i = PARTS - n
                        sp.dma_start(qrys[g][row:row + HD, :, :],
                                     qparts[b, heads, i * HD:(i + 1) * HD, :].rearrange("h r k -> r h k")
                                     ).then_inc(kq_loaded[g], 16)
                        row += HD
                sp.dma_start(vals[g][:, :, :, :].rearrange("p t h w -> p (t h w)"), vunits[b, g]
                             ).then_inc(v_loaded[g], 16)

            def place_shift(b, r):
                bb, g = vitem(b, r)
                sp.wait_ge(item_taken, LOOP_ITEMS * b + plan.turn_of[b if isinstance(b, int) else None, r] + 1)
                n = GROUP * QTILES
                for i in range(PARTS):
                    sp.dma_start(qrys[g][PROD + i:PROD + i + 1, :, :].rearrange("o h (t j) -> o (h t) j", j=P),
                                 negT[r % 2][i * n:(i + 1) * n, :]).then_inc(shift_placed[g], 16)

            sp.wait_ge(v_written, 16 * BATCHES)
            sp.wait_ge(kq_written, 16 * KQ_WRITES * BATCHES)
            for g in range(GROUPS):
                load_unit(0, g)
            place_shift(0, 0)
            place_shift(0, 1)
            with sp.Fori(0, BATCHES - 1) as b:
                for r in range(1, GROUPS + 1):
                    sp.wait_ge(pv_done, KTILES * (GROUPS * b + r))
                    load_unit(b + 1, r - 1)
                    place_shift(b, r + 1)
            b = BATCHES - 1
            for r in range(2, GROUPS):
                place_shift(b, r)

        @block.gpsimd
        def _(pool):
            pool.memset(ident[:, :], 0.0).then_inc(ident_cleared, 1)
            pool.memset(minus_half[:, :], -0.5).then_inc(ident_cleared, 1)
            pool.memset(eps[:, :], LN_EPS).then_inc(ident_cleared, 1)
            pool.wait_ge(ident_cleared, 3)
            pool.affine_select(out=ident[:, :], in_=ident[:, :], compare_op=ALU.not_equal, fill=1.0, base=0,
                               pattern=[[-1, P]], channel_multiplier=1).then_inc(ident_made, 1)
            pool.wait_ge(ident_made, 1)
            for g in range(GROUPS):
                pool.memset(keys[g][PROD:ROWS, :, :], 1.0).then_inc(ones_made, 1)
                pool.wait_ge(ones_made, g + 1)
            for t, v in ((bv_row, bv), (bo_row, bo), (g_row, ln_g), (b_row, ln_b)):
                pool.dma_start(t[:, :], v.partition_broadcast(P)).then_inc(rows_loaded, 16)
            pool.wait_ge(rows_loaded, 16 * ROWS_N)

            def residual(b):
                pool.dma_start(resid[:, :, :], x[b].rearrange("(t p) d -> p t d", p=P)).then_inc(resid_loaded, 16)
                pool.wait_ge(resid_loaded, 16 * (b + 1))
                for t in range(QTILES):
                    pool.tensor_tensor(resid[:, t, :], resid[:, t, :], bo_row[:, :], ALU.add
                                       ).then_inc(resid_ready, 1)

            def layernorm(b):
                for t in range(QTILES):
                    base = NORM_STEPS * (QTILES * b + t)
                    pool.wait_ge(mv_ready, QTILES * b + t + 1)
                    pool.tensor_tensor(rstd[:, t, 0:1], mv[:, t, 1:2], eps[:, :], ALU.add).then_inc(norm_step, 1)
                    pool.wait_ge(norm_step, base + 1)
                    pool.tensor_tensor(rstd[:, t, 1:2], rstd[:, t, 0:1], minus_half[:, :], ALU.pow
                                       ).then_inc(norm_step, 1)
                    pool.wait_ge(norm_step, base + 2)
                    if not is_first(b):
                        pool.wait_ge(out_written, 16 * QTILES * b)
                    for n, (src, by, op) in enumerate((
                            (y, mv[:, t, 0:1].to_broadcast([P, DIM]), ALU.subtract),
                            (z, rstd[:, t, 1:2].to_broadcast([P, DIM]), ALU.mult),
                            (z, g_row[:, :], ALU.mult), (z, b_row[:, :], ALU.add))):
                        pool.tensor_tensor(z[:, t, :], src[:, t, :], by, op).then_inc(norm_step, 1)
                        pool.wait_ge(norm_step, base + 3 + n)
                    pool.dma_start(out[b, t * P:(t + 1) * P, :], z[:, t, :]).then_inc(out_written, 16)

            residual(0)
            layernorm(0)
            residual(1)
            with pool.Fori(1, BATCHES - 1) as b:
                layernorm(b)
                residual(b + 1)
            layernorm(BATCHES - 1)
            pool.wait_ge(out_written, 16 * QTILES * BATCHES)

        @block.scalar
        def _(act):
            act.wait_ge(weights_loaded, 16 * WEIGHTS)

            def take_pieces(b):
                for n, (kind, h, c) in enumerate(PIECES):
                    if BY_DVE[n]:
                        continue
                    src = psum[:, n % BANKS, 0:CHUNKS[c]]
                    act.wait_ge(piece_made, NPIECES * b + n + 1)
                    if kind == "xt":
                        act.activation(xT[:, h, :], src, ACT.Copy).then_inc(act_took, 1)
                    elif kind == "ct":
                        act.activation(ctxT[:, h, c * BANK:c * BANK + CHUNKS[c]], src, ACT.Copy
                                       ).then_inc(act_took, 1)
                    elif kind == "k":
                        if not is_first(b):
                            act.wait_ge(split_step, 2 * HALVES * SPLITS * b)
                        act.activation(kf[:, h, c * BANK:c * BANK + CHUNKS[c]], src, ACT.Identity,
                                       bias=bk_col[:, h:h + 1]).then_inc(act_took, 1)
                    else:
                        act.activation(qf[:, h, :], src, ACT.Identity, bias=bq_col[:, h:h + 1]
                                       ).then_inc(act_took, 1)

            take_pieces(0)
            with act.Fori(1, BATCHES) as b:
                take_pieces(b)

            def unit(b, r, first=False):
                u = GROUPS * b + r
                for kt in range(KTILES):
                    s = KTILES * u + kt
                    rows = P if kt < FULL else REST
                    for p in range(2):
                        act.wait_ge(scores_ready, 2 * s + p + 1)
                        if not first or kt >= PBUFS:
                            act.wait_ge(pv_done, s - PBUFS + 1)
                        buf = (KTILES * r + kt) % PBUFS
                        act.activation(probs[0:rows, buf, p * 2 * BANK:(p + 1) * 2 * BANK],
                                       s_pair[p][0:rows, :], ACT.Exp, scale=SCALE).then_inc(probs_ready, 1)
                    if kt == 0 and not first:
                        copy_out(b, r - 1)

            def copy_out(b, r):
                act.wait_ge(pv_done, KTILES * (GROUPS * b + r + 1))
                if r == 0:
                    act.wait_ge(item_made, LOOP_ITEMS * b + plan.turned + 1)
                act.activation(o_out[:, r, :], o_bank, ACT.Copy).then_inc(o_copied, 1)

            unit(0, 0, first=True)
            with act.Fori(0, BATCHES - 1) as b:
                for r in range(1, GROUPS + 1):
                    unit(b, r)
            for r in range(1, GROUPS):
                unit(BATCHES - 1, r)
            copy_out(BATCHES - 1, GROUPS - 1)

        @block.vector
        def _(dve):
            dve.memset(zeros[:, :], 0.0).then_inc(consts_made, 1)
            dve.memset(v_out[:, :, :, :, :], 1.0).then_inc(consts_made, 1)
            for t in negpad:
                dve.memset(t[:, :], 0.0).then_inc(consts_made, 1)
            dve.wait_ge(ident_made, 1)
            dve.tensor_copy(identb[:, :], ident[:, :]).then_inc(consts_made, 1)
            dve.wait_ge(rows_loaded, 16 * ROWS_N)
            dve.wait_ge(consts_made, CONSTS)

            def split(b, n, m, src, dst, width, took):
                base = 2 * HALVES * SPLITS * b + (n * HALVES + m) * SPLITS
                dve.wait_ge(act_took, took)
                if not (is_first(b) and base == 0):
                    dve.wait_ge(split_step, base)
                if not is_first(b):
                    dve.wait_ge(kq_written, 16 * KQ_WRITES * b)
                rest = left[:, 0:width]
                dve.tensor_copy(dst[:, m, 0, :], src[:, m, :]).then_inc(split_step, 1)
                dve.wait_ge(split_step, base + 1)
                dve.tensor_tensor(rest, src[:, m, :], dst[:, m, 0, :], ALU.subtract).then_inc(split_step, 1)
                dve.wait_ge(split_step, base + 2)
                dve.tensor_copy(dst[:, m, 1, :], rest).then_inc(split_step, 1)
                dve.wait_ge(split_step, base + 3)
                dve.tensor_tensor(dst[:, m, 2, :], rest, dst[:, m, 1, :], ALU.subtract).then_inc(split_step, 1)

            def take_and_split(b):
                if not is_first(b):
                    dve.wait_ge(v_written, 16 * b)
                for n, (kind, t, _c) in enumerate(PIECES):
                    if not BY_DVE[n]:
                        continue
                    dve.wait_ge(piece_made, NPIECES * b + n + 1)
                    last = None
                    both = min(2, KTILES - t)
                    for i in range(both):
                        rows = P if t + i < FULL else REST
                        last = dve.tensor_tensor(
                            v_out[0:rows, :, t + i, :, 0:HD],
                            psum[0:rows, n % BANKS, i * DIM:(i + 1) * DIM].rearrange(
                                "p (g h d) -> p g h d", g=GROUPS, h=GROUP),
                            bv_row[0:rows, :].rearrange("p (g h d) -> p g h d", g=GROUPS, h=GROUP), ALU.add)
                    last.then_inc(dve_took, 1)
                for m in range(HALVES):
                    split(b, 0, m, kf, kp, KEYS, ACT_PIECES * b + TURNS + (m + 1) * len(CHUNKS))
                for m in range(HALVES):
                    split(b, 1, m, qf, qp, QUERIES, ACT_PIECES * b + TURNS + HALVES * len(CHUNKS) + m + 1)

            take_and_split(0)
            with dve.Fori(1, BATCHES) as b:
                take_and_split(b)

            def item(b, n, it):
                at = LOOP_ITEMS * b + n
                bank = ring[n % RING]
                dve.wait_ge(item_made, at + 1)
                if it[0] == "s":
                    _, r, h, j = it
                    if j < SMAX - 1:
                        t, c = divmod(j, len(CHUNKS) - 1)
                        dve.tensor_reduce(mx[r % 2][:, h, t, c:c + 1], bank, AX.X, ALU.max
                                          ).then_inc(item_taken, 1)
                    else:
                        dve.tensor_reduce(mx[r % 2][:, h, :, len(CHUNKS) - 1],
                                          bank[:, 0:QTILES * REST].rearrange("p (t k) -> p t k", t=QTILES),
                                          AX.X, ALU.max).then_inc(item_taken, 1)
                    if h == GROUP - 1 and j == SMAX - 1:
                        shifts(b, r, at)
                elif it[0] == "m":
                    r = it[1]
                    bb, g = vitem(b, r - 2)
                    if not (isinstance(bb, int) and bb < 0):
                        dve.wait_ge(shift_placed[g], 16 * PARTS * (bb + 1))
                    k = PARTS * GROUP * QTILES
                    dve.tensor_copy(negT[r % 2][:, :], bank.bitcast(BF16)[0:k, 0:P]).then_inc(item_taken, 1)
                elif it[0] == "o":
                    t = it[1]
                    o = bank.rearrange("p (h w) -> p h w", w=32)
                    dve.reciprocal(rden[:, t, :], o[:, :, HD]).then_inc(rden_ready, 1)
                    dve.wait_ge(rden_ready, QTILES * b + t + 1)
                    dve.tensor_tensor(o_norm[:, t, :, :], o[:, :, 0:HD],
                                      rden[:, t, :].unsqueeze(2).to_broadcast([P, HEADS, HD]), ALU.mult
                                      ).then_inc(item_taken, 1)
                elif it[0] == "n":
                    dve.tensor_copy(o_normT[:, 2 * it[1]:2 * it[1] + 2, :, :].rearrange("p t h q -> p (t h q)"),
                                    bank).then_inc(item_taken, 1)
                else:
                    t = it[1]
                    dve.wait_ge(resid_ready, QTILES * b + t + 1)
                    dve.tensor_tensor(y[:, t, :], bank[:, 0:DIM], resid[:, t, :], ALU.add
                                      ).then_inc(item_taken, 1)
                    dve.wait_ge(item_taken, at + 1)
                    dve.bn_stats(stats[:, t, :], y[:, t, :]).then_inc(stats_ready, 1)

            def shifts(b, r, at):
                n, base = r % 2, SHIFT_STEPS * (GROUPS * b + r)
                dve.wait_ge(item_taken, at + 1)
                dve.tensor_reduce(neg[n][:, :], mx[n][:, :, :, :].rearrange("p h t c -> p (h t) c"), AX.X,
                                  ALU.max, negate=True).then_inc(shift_step, 1)
                dve.wait_ge(shift_step, base + 1)
                dve.tensor_copy(negparts[n][:, 0, :], neg[n][:, :]).then_inc(shift_step, 1)
                dve.wait_ge(shift_step, base + 2)
                dve.tensor_tensor(negleft[n][:, :], neg[n][:, :], negparts[n][:, 0, :], ALU.subtract
                                  ).then_inc(shift_step, 1)
                dve.wait_ge(shift_step, base + 3)
                dve.tensor_copy(negparts[n][:, 1, :], negleft[n][:, :]).then_inc(shift_step, 1)
                dve.wait_ge(shift_step, base + 4)
                dve.tensor_tensor(negparts[n][:, 2, :], negleft[n][:, :], negparts[n][:, 1, :], ALU.subtract
                                  ).then_inc(shift_step, 1)

            def items(b, slots):
                before = None
                for slot in slots:
                    for n, it in slot:
                        if before is not None:
                            dve.wait_ge(stats_ready, QTILES * b + before + 1)
                        item(b, n, it)
                        if before is not None:
                            dve.bn_aggr(mv[:, before, :], stats[:, before, :]).then_inc(mv_ready, 1)
                        before = it[1] if it[0] == "y" else None
                if before is not None:
                    dve.wait_ge(stats_ready, QTILES * b + before + 1)
                    dve.bn_aggr(mv[:, before, :], stats[:, before, :]).then_inc(mv_ready, 1)

            items(0, [plan.prologue] + plan.unit0)
            with dve.Fori(0, BATCHES - 1) as b:
                for slots in plan.body:
                    items(b, slots)
            for slots in plan.tail:
                items(BATCHES - 1, slots)
            items(BATCHES - 1, [plan.ending])

        @block.tensor
        def _(pe):
            pe.wait_ge(weights_loaded, 16 * WEIGHTS)
            pe.wait_ge(consts_made, CONSTS)

            def bank_free(b, n):
                before = n - BANKS
                if before >= 0:
                    pb = b
                else:
                    before = n + (NPIECES - 1 - n) // BANKS * BANKS
                    pb = b - 1
                count = sum(BY_DVE[i] == BY_DVE[before] for i in range(before + 1))
                if isinstance(pb, int) and pb < 0:
                    return
                if BY_DVE[before]:
                    pe.wait_ge(dve_took, DVE_PIECES * pb + count)
                else:
                    pe.wait_ge(act_took, ACT_PIECES * pb + count)

            def project(b):
                for n, (kind, h, c) in enumerate(PIECES):
                    bank, width = psum[:, n % BANKS, :], CHUNKS[c]
                    bank_free(b, n)
                    if n == 0:
                        pe.wait_ge(x_loaded, 16 * (b + 1))
                    if n == HALVES:
                        pe.wait_ge(ctx_loaded, 32 * (b + 1))
                    if n == TURNS:
                        pe.wait_ge(act_took, ACT_PIECES * b + TURNS)
                    if kind == "xt":
                        for t in range(QTILES):
                            mm = pe.transpose(bank[:, t * P:(t + 1) * P], x_in[:, t, h * P:(h + 1) * P], ident[:, :])
                    elif kind == "ct":
                        for i in range(0, width, P):
                            w = min(P, width - i)
                            mm = pe.transpose(bank[:, i:i + w], ctx_in[0:w, (c * BANK + i) // P, h * P:(h + 1) * P],
                                              ident[0:w, 0:w])
                    elif kind == "v":
                        for i in range(min(2, KTILES - h)):
                            w = P if h + i < FULL else REST
                            for k in range(HALVES):
                                mm = pe.matmul(bank[0:w, i * DIM:(i + 1) * DIM],
                                               ctxT[:, k, (h + i) * P:(h + i) * P + w], wv[:, k, :],
                                               start=(k == 0), stop=(k == HALVES - 1))
                    else:
                        w, src = (wk, ctxT) if kind == "k" else (wq, xT)
                        for k in range(HALVES):
                            mm = pe.matmul(bank[:, 0:width], w[:, k, h * P:(h + 1) * P],
                                           src[:, k, c * BANK:c * BANK + width],
                                           start=(k == 0), stop=(k == HALVES - 1))
                    mm.then_inc(piece_made, 1)

            project(0)
            with pe.Fori(1, BATCHES) as b:
                project(b)
            pe.wait_ge(act_took, ACT_PIECES * BATCHES)
            pe.wait_ge(dve_took, DVE_PIECES * BATCHES)
            pe.matmul(o_bank, zeros[0:PROD, 0:P], zeros[0:PROD, :], start=True, stop=True)

            def item(b, n, it):
                at = LOOP_ITEMS * b + n
                bank = ring[n % RING]
                if not (isinstance(b, int) and at < RING):
                    pe.wait_ge(item_taken, at - RING + 1)
                if it[0] == "s":
                    _, r, h, j = it
                    bb, g = vitem(b, r)
                    if h == 0 and j == 0:
                        pe.wait_ge(kq_loaded[g], 16 * KQ_DMAS * (bb + 1))
                    if j < SMAX - 1:
                        t, c = divmod(j, len(CHUNKS) - 1)
                        mm = pe.matmul(bank, qrys[g][0:PROD, h, t * P:(t + 1) * P],
                                       keys[g][0:PROD, h, c * BANK:(c + 1) * BANK], start=True, stop=True)
                    else:
                        for t in range(QTILES):
                            mm = pe.matmul(bank[:, t * REST:(t + 1) * REST], qrys[g][0:PROD, h, t * P:(t + 1) * P],
                                           keys[g][0:PROD, h, KEYS - REST:KEYS], start=True, stop=True)
                elif it[0] == "m":
                    r = it[1]
                    pe.wait_ge(shift_step, SHIFT_STEPS * (GROUPS * b + r + 1))
                    mm = pe.transpose(bank.bitcast(BF16)[:, 0:P], negpad[r % 2][:, :], identb[:, :])
                elif it[0] == "o":
                    t = it[1]
                    pe.wait_ge(o_copied, GROUPS * (b + 1))
                    for g in range(GROUPS):
                        mm = pe.transpose(bank[:, g * P:(g + 1) * P], o_out[:, g, t * P:(t + 1) * P], ident[:, :])
                elif it[0] == "n":
                    pe.wait_ge(item_taken, LOOP_ITEMS * b + ending_at[("o", 2 * it[1] + 1)] + 1)
                    for i in range(2):
                        src = o_norm[:, 2 * it[1] + i, :, :].rearrange("p h d -> p (h d)")
                        for h in range(HALVES):
                            mm = pe.transpose(bank[:, (i * HALVES + h) * P:(i * HALVES + h + 1) * P],
                                              src[:, h * P:(h + 1) * P], ident[:, :])
                else:
                    t = it[1]
                    pe.wait_ge(item_taken, LOOP_ITEMS * b + ending_at[("n", t // 2)] + 1)
                    for h in range(HALVES):
                        mm = pe.matmul(bank[:, 0:DIM], o_normT[:, t, h, :], wo[:, h, :],
                                       start=(h == 0), stop=(h == HALVES - 1))
                mm.then_inc(item_made, 1)

            def scores(b, r, kt, p):
                u = GROUPS * b + r
                s = KTILES * u + kt
                bb, g = vitem(b, r)
                if not (isinstance(u, int) and s == 0):
                    pe.wait_ge(probs_ready, 2 * s + p - 1)
                if kt == 0 and p == 0:
                    pe.wait_ge(ones_made, GROUPS)
                    pe.wait_ge(shift_placed[g], 16 * PARTS * (bb + 1))
                w = P if kt < FULL else REST
                for i in range(2):
                    h = 2 * p + i
                    mm = pe.matmul(s_bank[p][i][0:w, :], keys[g][:, h, kt * P:kt * P + w], qrys[g][:, h, :],
                                   start=True, stop=True)
                mm.then_inc(scores_ready, 1)

            def times_v(b, r, kt):
                u = GROUPS * b + r
                s = KTILES * u + kt
                bb, g = vitem(b, r)
                pe.wait_ge(probs_ready, 2 * s + 2)
                if kt == 0:
                    pe.wait_ge(v_loaded[g], 16 * V_DMAS * (bb + 1))
                    pe.wait_ge(o_copied, u)
                w = P if kt < FULL else REST
                buf = (KTILES * r + kt) % PBUFS
                for h in range(GROUP):
                    mm = pe.matmul(o_bank[32 * h:32 * h + VW, :], vals[g][0:w, kt, h, :],
                                   probs[0:w, buf, h * BANK:(h + 1) * BANK],
                                   start=(kt == 0), stop=(kt == KTILES - 1))
                mm.then_inc(pv_done, 1)

            def unit(b, r, slots, first=False):
                for kt in range(KTILES):
                    for p in range(2):
                        scores(b, r, kt, p)
                        for n, it in slots[2 * kt + p]:
                            item(b, n, it)
                    if kt:
                        times_v(b, r, kt - 1)
                    elif not first:
                        times_v(b, r - 1, KTILES - 1)

            ending_at = {it: n for slots in plan.body for slot in slots for n, it in slot}
            for n, it in plan.prologue:
                item(0, n, it)
            unit(0, 0, plan.unit0, first=True)
            with pe.Fori(0, BATCHES - 1) as b:
                for r in range(1, GROUPS + 1):
                    unit(b, r, plan.body[r - 1])
            for r in range(1, GROUPS):
                unit(BATCHES - 1, r, plan.tail[r - 1])
            times_v(BATCHES - 1, GROUPS - 1, KTILES - 1)
            ending_at = {it: n for n, it in plan.ending}
            for n, it in plan.ending:
                item(BATCHES - 1, n, it)


_INS = ["x", "ctx_1024", "L0_xattn_Wq", "L0_xattn_bq", "L0_xattn_Wk", "L0_xattn_bk", "L0_xattn_Wv", "L0_xattn_bv",
        "L0_xattn_Wo", "L0_xattn_bo", "L0_xattn_ln_g", "L0_xattn_ln_b"]


def kernel(**inputs):
    import numpy as np
    import concourse.bacc as bacc
    from concourse.bass_utils import run_bass_kernel_spmd

    nc = bacc.Bacc("TRN2", target_bir_lowering=False, num_devices=1)
    arrays, args = {}, []
    for name in _INS:
        a = np.ascontiguousarray(inputs[name])
        arrays[f"in_{name}"] = a
        args.append(nc.dram_tensor(f"in_{name}", a.shape, mybir.dt.from_np(a.dtype), kind="ExternalInput").ap())
    out = nc.dram_tensor("out_x", (BATCHES, QUERIES, DIM), F32, kind="ExternalOutput").ap()
    xattn_kernel(nc, *args, out)
    r = run_bass_kernel_spmd(nc, [arrays], core_ids=[0])
    return r.results[0]["out_x"]
```

```python
from contextlib import ExitStack

import concourse.bass as bass
from concourse import mybir

F32 = mybir.dt.float32
BF16 = mybir.dt.bfloat16
ALU = mybir.AluOpType
ACT = mybir.ActivationFunctionType
AX = mybir.AxisListType

P = 128
BANK = 512
BATCHES, QUERIES, DIM = 8, 512, 256
KEYS = 1601
HEADS, HD = 16, 16
LN_EPS = 1e-5

HALVES = DIM // P
GROUP = 4
GROUPS = HEADS // GROUP
UNITS = BATCHES * GROUPS
QTILES = QUERIES // P
FULL = KEYS // P
REST = KEYS - FULL * P
KTILES = FULL + 1
CHUNKS = [BANK] * (KEYS // BANK) + [KEYS % BANK]
assert CHUNKS[-1] == REST and QUERIES == BANK
PARTS = 3
PROD = 6 * HD
ROWS = PROD + PARTS
KPITCH = KEYS + 7
VW = HD + 1
SCALE = 1.0 / HD ** 0.5

PIECES = ([("xt", h, 0) for h in range(HALVES)]
          + [("ct", h, c) for c in range(len(CHUNKS)) for h in range(HALVES)]
          + [("q", m, 0) for m in range(HALVES)]
          + [("v", t, 0) for t in range(0, KTILES, 2)]
          + [("k", m, c) for m in range(HALVES) for c in range(len(CHUNKS))])
NPIECES = len(PIECES)
TURNS = sum(p[0] in ("xt", "ct") for p in PIECES)
BY_DVE = [p[0] == "v" for p in PIECES]
ACT_PIECES, DVE_PIECES = NPIECES - sum(BY_DVE), sum(BY_DVE)
BANKS = 8
SPLITS = 4

RING = 3
SMAX = QTILES * (len(CHUNKS) - 1) + 1
PERIOD = GROUP * SMAX + 1
LEAD = [20, 12, 15, 18]
TURN_AT = 7
PBUFS = 4
NORM_LAG = 6
SHIFT_STEPS = 5


def period(r):
    items = [("s", r, h, j) for h in range(GROUP) for j in range(SMAX)]
    return items[:TURN_AT] + [("m", r - 1)] + items[TURN_AT:]


ENDING = ([(7 + 2 * t, ("o", t)) for t in range(QTILES)]
          + [(16 + 2 * t, ("n", t // 2)) for t in range(0, QTILES, 2)]
          + [(23 + 4 * t, ("y", t)) for t in range(QTILES)])
LOOP_ITEMS = GROUPS * PERIOD + len(ENDING)
assert LOOP_ITEMS % RING == 0 and (GROUPS * KTILES) % PBUFS == 0


def spread(items, ending):
    slots = [[] for _ in range(GROUP * KTILES)]
    for n, it in enumerate(items):
        slots[n * len(slots) // len(items)].append(it)
    for quarter, it in ending:
        slots[quarter].insert(0, it)
    return slots


def is_first(b):
    return isinstance(b, int) and b == 0


class Plan:

    def __init__(self):
        first = [it for it in period(0) if it[0] == "s"] + period(1)[:LEAD[1]]
        self.count = 0
        self.prologue = self.numbered([first])[0]
        self.unit0 = self.unit(0, [], lead=LEAD[1])
        self.loop_start = self.count
        self.body = [self.unit(r, ENDING if r == GROUPS else []) for r in range(1, GROUPS + 1)]
        assert self.count == self.loop_start + LOOP_ITEMS
        self.count = self.loop_start
        self.tail = [self.unit(1, []), self.unit(2, [], last=True), self.unit(3, [], none=True)]
        self.ending = self.numbered([[it for _, it in ENDING]])[0]
        self.turn_of = {}
        for b, units in ((0, [[self.prologue], self.unit0]), (None, self.body), (BATCHES - 1, self.tail)):
            self.turn_of |= {(b, it[1]): n for slots in units for slot in slots for n, it in slot if it[0] == "m"}
        at = {it: n for slots in self.body for slot in slots for n, it in slot}
        self.turned = at[("o", QTILES - 1)] - LOOP_ITEMS

    def numbered(self, slots):
        out = []
        for slot in slots:
            out.append([(self.count + n, it) for n, it in enumerate(slot)])
            self.count += len(slot)
        return out

    def unit(self, r, ending, lead=None, last=False, none=False):
        lead = LEAD[r % GROUPS] if lead is None else lead
        items = period(r + 1)[lead:] + period(r + 2)[:LEAD[(r + 1) % GROUPS]]
        if last:
            items = period(r + 1)[lead:] + [("m", r + 1)]
        return self.numbered(spread([] if none else items, ending))


def xattn_kernel(nc, x, ctx, Wq, bq, Wk, bk, Wv, bv, Wo, bo, ln_g, ln_b, out):
    plan = Plan()
    kparts = nc.dram_tensor("kparts", [BATCHES, HEADS, PARTS * HD, KEYS], BF16, kind="Internal").ap()
    qparts = nc.dram_tensor("qparts", [BATCHES, HEADS, PARTS * HD, QUERIES], BF16, kind="Internal").ap()
    vunits = nc.dram_tensor("vunits", [BATCHES, GROUPS, P, KTILES * GROUP * VW], F32, kind="Internal").ap()

    with ExitStack() as stack:
        def sb(name, shape, dt):
            return stack.enter_context(nc.sbuf_tensor(name, shape, dt))

        def sem(name):
            return stack.enter_context(nc.semaphore(name))

        ident = sb("ident", [P, P], F32)
        identb = sb("identb", [P, P], BF16)
        zeros = sb("zeros", [P, BANK], BF16)
        wq, wk, wv, wo = (sb(n, [P, HALVES, DIM], F32) for n in ("wq", "wk", "wv", "wo"))
        bq_col, bk_col = (sb(n, [P, HALVES], F32) for n in ("bq_col", "bk_col"))
        bv_row, bo_row, g_row, b_row = (sb(n, [P, DIM], F32) for n in ("bv_row", "bo_row", "g_row", "b_row"))
        minus_half = sb("minus_half", [P, 1], F32)
        eps = sb("eps", [P, 1], F32)
        probs = sb("probs", [P, PBUFS, GROUP * BANK], F32)
        flat = probs[:, :, :].rearrange("p a b -> p (a b)")
        ctx_in = flat[:, 0:KTILES * DIM].rearrange("p (t d) -> p t d", t=KTILES)
        ctxT = flat[:, KTILES * DIM:KTILES * DIM + HALVES * KEYS].rearrange("p (h k) -> p h k", h=HALVES)
        x_in = sb("x_in", [P, QTILES, DIM], F32)
        xT = sb("xT", [P, HALVES, QUERIES], F32)
        kf = sb("kf", [P, HALVES, KEYS], F32)
        qf = sb("qf", [P, HALVES, QUERIES], F32)
        left = sb("left", [P, KEYS], F32)
        kp = sb("kp", [P, HALVES, PARTS, KEYS], BF16)
        qp = sb("qp", [P, HALVES, PARTS, QUERIES], BF16)
        v_out = sb("v_out", [P, GROUPS, KTILES, GROUP, VW], F32)
        keys = [sb(f"keys{g}", [ROWS, GROUP, KPITCH], BF16) for g in range(GROUPS)]
        qrys = [sb(f"qrys{g}", [ROWS, GROUP, QUERIES], BF16) for g in range(GROUPS)]
        vals = [sb(f"vals{g}", [P, KTILES, GROUP, VW], F32) for g in range(GROUPS)]
        mx = [sb(f"mx{n}", [P, GROUP, QTILES, len(CHUNKS)], F32) for n in range(2)]
        neg = [sb(f"neg{n}", [P, GROUP * QTILES], F32) for n in range(2)]
        negleft = [sb(f"negleft{n}", [P, GROUP * QTILES], F32) for n in range(2)]
        negpad = [sb(f"negpad{n}", [P, P], BF16) for n in range(2)]
        negparts = [t[:, 0:PARTS * GROUP * QTILES].rearrange("p (i n) -> p i n", i=PARTS) for t in negpad]
        negT = [sb(f"negT{n}", [PARTS * GROUP * QTILES, P], BF16) for n in range(2)]
        def over(tensor, start, *dims):
            n = 1
            for d in dims:
                n *= d
            names = "abc"[:len(dims)]
            return tensor[:, start:start + n].rearrange(
                f"p ({' '.join(names)}) -> p {' '.join(names)}", **dict(zip(names, dims)))

        kf_flat = kf[:, :, :].rearrange("p h k -> p (h k)")
        o_out = over(v_out[:, :, :, :, :].rearrange("p g t h w -> p (g t h w)"), 0, GROUPS, QUERIES)
        rden = sb("rden", [P, QTILES, HEADS], F32)
        o_norm = over(kf_flat, 0, QTILES, HEADS, HD)
        o_normT = over(kf_flat, QTILES * DIM, QTILES, HALVES, P)
        resid = sb("resid", [P, QTILES, DIM], F32)
        y = over(kf_flat, 2 * QTILES * DIM, QTILES, DIM)
        stats = sb("stats", [P, QTILES, 6], F32)
        mv = sb("mv", [P, QTILES, 2], F32)
        rstd = sb("rstd", [P, QTILES, 2], F32)
        z = over(left, 0, QTILES, DIM)

        psum = stack.enter_context(nc.psum_tensor("psum", [P, BANKS, BANK], F32))
        s_bank = [[psum[:, 2 * p + n, :] for n in range(2)] for p in range(2)]
        s_pair = [psum[:, 2 * p:2 * p + 2, :].rearrange("p a b -> p (a b)") for p in range(2)]
        ring = [psum[:, 4 + n, :] for n in range(RING)]
        o_bank = psum[:, BANKS - 1, :]

        weights_loaded = sem("weights_loaded")
        rows_loaded = sem("rows_loaded")
        ident_cleared = sem("ident_cleared")
        ident_made = sem("ident_made")
        consts_made = sem("consts_made")
        ones_made = sem("ones_made")
        x_loaded = sem("x_loaded")
        ctx_loaded = sem("ctx_loaded")
        piece_made = sem("piece_made")
        act_took = sem("act_took")
        dve_took = sem("dve_took")
        split_step = sem("split_step")
        v_written = sem("v_written")
        kq_written = sem("kq_written")
        kq_loaded = [sem(f"kq_loaded{g}") for g in range(GROUPS)]
        v_loaded = [sem(f"v_loaded{g}") for g in range(GROUPS)]
        item_made = sem("item_made")
        item_taken = sem("item_taken")
        shift_step = sem("shift_step")
        shift_placed = [sem(f"shift_placed{g}") for g in range(GROUPS)]
        scores_ready = sem("scores_ready")
        probs_ready = sem("probs_ready")
        pv_done = sem("pv_done")
        o_copied = sem("o_copied")
        rden_ready = sem("rden_ready")
        y_ready = sem("y_ready")
        stats_ready = sem("stats_ready")
        mv_ready = sem("mv_ready")
        resid_loaded = sem("resid_loaded")
        resid_ready = sem("resid_ready")
        norm_step = sem("norm_step")
        z_ready = sem("z_ready")
        out_written = sem("out_written")
        KQ_DMAS, V_DMAS = 9, 1
        KQ_WRITES = 2 * HALVES * PARTS
        WEIGHTS, ROWS_N = 6, 4
        NORM_STEPS = 4
        CONSTS = 2 + 2 + 1

        def vitem(b, r):
            return b + r // GROUPS, r % GROUPS

        block = stack.enter_context(nc.Block())

        @block.sync
        def _(sp):
            for t, w in ((wq, Wq), (wk, Wk), (wv, Wv), (wo, Wo)):
                sp.dma_start(t[:, :, :], w.rearrange("(h p) n -> p h n", p=P)).then_inc(weights_loaded, 16)
            with nc.allow_non_contiguous_dma("two columns of biases"):
                for t, v in ((bq_col, bq), (bk_col, bk)):
                    sp.dma_start(t[:, :], v.rearrange("(h p) -> p h", p=P)).then_inc(weights_loaded, 16)

            def load_inputs(b):
                sp.dma_start(x_in[:, :, :], x[b].rearrange("(t p) d -> p t d", p=P)).then_inc(x_loaded, 16)
                sp.dma_start(ctx_in[:, 0:FULL, :],
                             ctx[b, 0:FULL * P, :].rearrange("(t p) d -> p t d", p=P)).then_inc(ctx_loaded, 16)
                sp.dma_start(ctx_in[0:REST, FULL, :], ctx[b, FULL * P:KEYS, :]).then_inc(ctx_loaded, 16)

            def store_parts(b):
                for n, (src, dst) in enumerate(((qp, qparts), (kp, kparts))):
                    if n:
                        sp.wait_ge(dve_took, DVE_PIECES * (b + 1))
                        sp.dma_start(vunits[b].rearrange("g p n -> p g n"),
                                     v_out[:, :, :, :, :].rearrange("p g t h w -> p g (t h w)")
                                     ).then_inc(v_written, 16)
                    for m in range(HALVES):
                        sp.wait_ge(split_step, 2 * HALVES * SPLITS * b + (n * HALVES + m + 1) * SPLITS)
                        for i in range(PARTS):
                            sp.dma_start(
                                dst[b, m * HEADS // HALVES:(m + 1) * HEADS // HALVES, i * HD:(i + 1) * HD, :],
                                src[:, m, i, :]).then_inc(kq_written, 16)

            load_inputs(0)
            with sp.Fori(0, BATCHES - 1) as b:
                sp.wait_ge(piece_made, NPIECES * b + TURNS)
                load_inputs(b + 1)
                store_parts(b)

            def load_unit(b, g):
                heads = slice(g * GROUP, (g + 1) * GROUP)
                row = 0
                for n in (3, 2, 1):
                    sp.dma_start(keys[g][row:row + n * HD, :, 0:KEYS],
                                 kparts[b, heads, 0:n * HD, :].rearrange("h r k -> r h k")
                                 ).then_inc(kq_loaded[g], 16)
                    for _ in range(n):
                        i = PARTS - n
                        sp.dma_start(qrys[g][row:row + HD, :, :],
                                     qparts[b, heads, i * HD:(i + 1) * HD, :].rearrange("h r k -> r h k")
                                     ).then_inc(kq_loaded[g], 16)
                        row += HD
                sp.dma_start(vals[g][:, :, :, :].rearrange("p t h w -> p (t h w)"), vunits[b, g]
                             ).then_inc(v_loaded[g], 16)

            def place_shift(b, r):
                bb, g = vitem(b, r)
                sp.wait_ge(item_taken, LOOP_ITEMS * b + plan.turn_of[b if isinstance(b, int) else None, r] + 1)
                n = GROUP * QTILES
                for i in range(PARTS):
                    sp.dma_start(qrys[g][PROD + i:PROD + i + 1, :, :].rearrange("o h (t j) -> o (h t) j", j=P),
                                 negT[r % 2][i * n:(i + 1) * n, :]).then_inc(shift_placed[g], 16)

            sp.wait_ge(v_written, 16 * (BATCHES - 1))
            sp.wait_ge(kq_written, 16 * KQ_WRITES * (BATCHES - 1))
            for g in range(GROUPS):
                load_unit(0, g)
            store_parts(BATCHES - 1)
            sp.wait_ge(v_written, 16 * BATCHES)
            sp.wait_ge(kq_written, 16 * KQ_WRITES * BATCHES)
            place_shift(0, 0)
            place_shift(0, 1)
            with sp.Fori(0, BATCHES - 1) as b:
                for r in range(1, GROUPS + 1):
                    sp.wait_ge(pv_done, KTILES * (GROUPS * b + r))
                    load_unit(b + 1, r - 1)
                    place_shift(b, r + 1)
            b = BATCHES - 1
            for r in range(2, GROUPS):
                place_shift(b, r)

        @block.gpsimd
        def _(pool):
            pool.memset(ident[:, :], 0.0).then_inc(ident_cleared, 1)
            pool.memset(minus_half[:, :], -0.5).then_inc(ident_cleared, 1)
            pool.memset(eps[:, :], LN_EPS).then_inc(ident_cleared, 1)
            pool.wait_ge(ident_cleared, 3)
            pool.affine_select(out=ident[:, :], in_=ident[:, :], compare_op=ALU.not_equal, fill=1.0, base=0,
                               pattern=[[-1, P]], channel_multiplier=1).then_inc(ident_made, 1)
            pool.wait_ge(ident_made, 1)
            for g in range(GROUPS):
                pool.memset(keys[g][PROD:ROWS, :, :], 1.0).then_inc(ones_made, 1)
                pool.wait_ge(ones_made, g + 1)
            for t, v in ((bv_row, bv), (bo_row, bo), (g_row, ln_g), (b_row, ln_b)):
                pool.dma_start(t[:, :], v.partition_broadcast(P)).then_inc(rows_loaded, 16)
            pool.wait_ge(rows_loaded, 16 * ROWS_N)

            def residual(b):
                pool.dma_start(resid[:, :, :], x[b].rearrange("(t p) d -> p t d", p=P)).then_inc(resid_loaded, 16)
                pool.wait_ge(resid_loaded, 16 * (b + 1))
                for t in range(QTILES):
                    pool.tensor_tensor(resid[:, t, :], resid[:, t, :], bo_row[:, :], ALU.add
                                       ).then_inc(resid_ready, 1)

            def layernorm(b):
                for t in range(QTILES):
                    base = NORM_STEPS * QTILES * b + 2 * t
                    pool.wait_ge(mv_ready, QTILES * b + t + 1)
                    pool.tensor_tensor(rstd[:, t, 0:1], mv[:, t, 1:2], eps[:, :], ALU.add).then_inc(norm_step, 1)
                    pool.wait_ge(norm_step, base + 1)
                    pool.tensor_tensor(rstd[:, t, 1:2], rstd[:, t, 0:1], minus_half[:, :], ALU.pow
                                       ).then_inc(norm_step, 1)
                for t in range(QTILES):
                    base = NORM_STEPS * QTILES * b + 2 * QTILES + 2 * t
                    pool.wait_ge(z_ready, QTILES * b + t + 1)
                    pool.tensor_tensor(z[:, t, :], z[:, t, :], g_row[:, :], ALU.mult).then_inc(norm_step, 1)
                    pool.wait_ge(norm_step, base + 1)
                    pool.tensor_tensor(z[:, t, :], z[:, t, :], b_row[:, :], ALU.add).then_inc(norm_step, 1)
                    pool.wait_ge(norm_step, base + 2)
                    pool.dma_start(out[b, t * P:(t + 1) * P, :], z[:, t, :]).then_inc(out_written, 16)

            residual(0)
            with pool.Fori(0, BATCHES - 1) as b:
                layernorm(b)
                pool.wait_ge(out_written, 16 * QTILES * (b + 1))
                residual(b + 1)
            layernorm(BATCHES - 1)
            pool.wait_ge(out_written, 16 * QTILES * BATCHES)

        @block.scalar
        def _(act):
            act.wait_ge(weights_loaded, 16 * WEIGHTS)

            def take_pieces(b):
                for n, (kind, h, c) in enumerate(PIECES):
                    if BY_DVE[n]:
                        continue
                    src = psum[:, n % BANKS, 0:CHUNKS[c]]
                    act.wait_ge(piece_made, NPIECES * b + n + 1)
                    if kind == "xt":
                        act.activation(xT[:, h, :], src, ACT.Copy).then_inc(act_took, 1)
                    elif kind == "ct":
                        act.activation(ctxT[:, h, c * BANK:c * BANK + CHUNKS[c]], src, ACT.Copy
                                       ).then_inc(act_took, 1)
                    elif kind == "k":
                        if not is_first(b):
                            act.wait_ge(split_step, 2 * HALVES * SPLITS * b)
                        act.activation(kf[:, h, c * BANK:c * BANK + CHUNKS[c]], src, ACT.Identity,
                                       bias=bk_col[:, h:h + 1]).then_inc(act_took, 1)
                    else:
                        if not is_first(b):
                            act.wait_ge(split_step, 2 * HALVES * SPLITS * b)
                        act.activation(qf[:, h, :], src, ACT.Identity, bias=bq_col[:, h:h + 1]
                                       ).then_inc(act_took, 1)

            take_pieces(0)
            with act.Fori(1, BATCHES) as b:
                take_pieces(b)

            def unit(b, r, first=False):
                u = GROUPS * b + r
                for kt in range(KTILES):
                    s = KTILES * u + kt
                    rows = P if kt < FULL else REST
                    for p in range(2):
                        act.wait_ge(scores_ready, 2 * s + p + 1)
                        if not first or kt >= PBUFS:
                            act.wait_ge(pv_done, s - PBUFS + 1)
                        buf = (KTILES * r + kt) % PBUFS
                        act.activation(probs[0:rows, buf, p * 2 * BANK:(p + 1) * 2 * BANK],
                                       s_pair[p][0:rows, :], ACT.Exp, scale=SCALE).then_inc(probs_ready, 1)
                    if kt == 0 and not first:
                        copy_out(b, r - 1)

            def copy_out(b, r):
                act.wait_ge(pv_done, KTILES * (GROUPS * b + r + 1))
                if r == 0:
                    act.wait_ge(item_made, LOOP_ITEMS * b + plan.turned + 1)
                act.activation(o_out[:, r, :], o_bank, ACT.Copy).then_inc(o_copied, 1)

            unit(0, 0, first=True)
            with act.Fori(0, BATCHES - 1) as b:
                for r in range(1, GROUPS + 1):
                    unit(b, r)
            for r in range(1, GROUPS):
                unit(BATCHES - 1, r)
            copy_out(BATCHES - 1, GROUPS - 1)

        @block.vector
        def _(dve):
            dve.memset(zeros[:, :], 0.0).then_inc(consts_made, 1)
            dve.memset(v_out[:, :, :, :, :], 1.0).then_inc(consts_made, 1)
            for t in negpad:
                dve.memset(t[:, :], 0.0).then_inc(consts_made, 1)
            dve.wait_ge(ident_made, 1)
            dve.tensor_copy(identb[:, :], ident[:, :]).then_inc(consts_made, 1)
            dve.wait_ge(rows_loaded, 16 * ROWS_N)
            dve.wait_ge(consts_made, CONSTS)

            def split(b, n, m, src, dst, width, took):
                base = 2 * HALVES * SPLITS * b + (n * HALVES + m) * SPLITS
                dve.wait_ge(act_took, took)
                if not (is_first(b) and base == 0):
                    dve.wait_ge(split_step, base)
                if not is_first(b):
                    dve.wait_ge(kq_written, 16 * KQ_WRITES * b)
                rest = left[:, 0:width]
                dve.tensor_copy(dst[:, m, 0, :], src[:, m, :]).then_inc(split_step, 1)
                dve.wait_ge(split_step, base + 1)
                dve.tensor_tensor(rest, src[:, m, :], dst[:, m, 0, :], ALU.subtract).then_inc(split_step, 1)
                dve.wait_ge(split_step, base + 2)
                dve.tensor_copy(dst[:, m, 1, :], rest).then_inc(split_step, 1)
                dve.wait_ge(split_step, base + 3)
                dve.tensor_tensor(dst[:, m, 2, :], rest, dst[:, m, 1, :], ALU.subtract).then_inc(split_step, 1)

            def take_and_split(b):
                for m in range(HALVES):
                    split(b, 0, m, qf, qp, QUERIES, ACT_PIECES * b + TURNS + m + 1)
                if not is_first(b):
                    dve.wait_ge(v_written, 16 * b)
                for n, (kind, t, _c) in enumerate(PIECES):
                    if not BY_DVE[n]:
                        continue
                    dve.wait_ge(piece_made, NPIECES * b + n + 1)
                    last = None
                    both = min(2, KTILES - t)
                    for i in range(both):
                        rows = P if t + i < FULL else REST
                        last = dve.tensor_tensor(
                            v_out[0:rows, :, t + i, :, 0:HD],
                            psum[0:rows, n % BANKS, i * DIM:(i + 1) * DIM].rearrange(
                                "p (g h d) -> p g h d", g=GROUPS, h=GROUP),
                            bv_row[0:rows, :].rearrange("p (g h d) -> p g h d", g=GROUPS, h=GROUP), ALU.add)
                    last.then_inc(dve_took, 1)
                for m in range(HALVES):
                    split(b, 1, m, kf, kp, KEYS, ACT_PIECES * b + TURNS + HALVES + (m + 1) * len(CHUNKS))

            take_and_split(0)
            with dve.Fori(1, BATCHES) as b:
                take_and_split(b)

            def item(b, n, it):
                at = LOOP_ITEMS * b + n
                bank = ring[n % RING]
                dve.wait_ge(item_made, at + 1)
                if it[0] == "s":
                    _, r, h, j = it
                    if j < SMAX - 1:
                        t, c = divmod(j, len(CHUNKS) - 1)
                        dve.tensor_reduce(mx[r % 2][:, h, t, c:c + 1], bank, AX.X, ALU.max
                                          ).then_inc(item_taken, 1)
                    else:
                        dve.tensor_reduce(mx[r % 2][:, h, :, len(CHUNKS) - 1],
                                          bank[:, 0:QTILES * REST].rearrange("p (t k) -> p t k", t=QTILES),
                                          AX.X, ALU.max).then_inc(item_taken, 1)
                elif it[0] == "m":
                    r = it[1]
                    bb, g = vitem(b, r - 2)
                    if not (isinstance(bb, int) and bb < 0):
                        dve.wait_ge(shift_placed[g], 16 * PARTS * (bb + 1))
                    k = PARTS * GROUP * QTILES
                    dve.tensor_copy(negT[r % 2][:, :], bank.bitcast(BF16)[0:k, 0:P]).then_inc(item_taken, 1)
                elif it[0] == "o":
                    t = it[1]
                    o = bank.rearrange("p (h w) -> p h w", w=32)
                    dve.reciprocal(rden[:, t, :], o[:, :, HD]).then_inc(rden_ready, 1)
                    dve.wait_ge(rden_ready, QTILES * b + t + 1)
                    dve.tensor_tensor(o_norm[:, t, :, :], o[:, :, 0:HD],
                                      rden[:, t, :].unsqueeze(2).to_broadcast([P, HEADS, HD]), ALU.mult
                                      ).then_inc(item_taken, 1)
                elif it[0] == "n":
                    dve.tensor_copy(o_normT[:, 2 * it[1]:2 * it[1] + 2, :, :].rearrange("p t h q -> p (t h q)"),
                                    bank).then_inc(item_taken, 1)
                else:
                    t = it[1]
                    dve.wait_ge(resid_ready, QTILES * b + t + 1)
                    dve.tensor_tensor(y[:, t, :], bank[:, 0:DIM], resid[:, t, :], ALU.add
                                      ).then_inc(item_taken, 1)
                    dve.wait_ge(item_taken, at + 1)
                    dve.bn_stats(stats[:, t, :], y[:, t, :]).then_inc(stats_ready, 1)

            def shift(b, r, step):
                n = r % 2
                if step:
                    dve.wait_ge(shift_step, SHIFT_STEPS * (GROUPS * b + r) + step)
                else:
                    dve.wait_ge(item_taken, LOOP_ITEMS * b + last_max[r] + 1)
                if step == 0:
                    made = dve.tensor_reduce(neg[n][:, :], mx[n][:, :, :, :].rearrange("p h t c -> p (h t) c"), AX.X,
                                             ALU.max, negate=True)
                elif step == 1:
                    made = dve.tensor_copy(negparts[n][:, 0, :], neg[n][:, :])
                elif step == 2:
                    made = dve.tensor_tensor(negleft[n][:, :], neg[n][:, :], negparts[n][:, 0, :], ALU.subtract)
                elif step == 3:
                    made = dve.tensor_copy(negparts[n][:, 1, :], negleft[n][:, :])
                else:
                    made = dve.tensor_tensor(negparts[n][:, 2, :], negleft[n][:, :], negparts[n][:, 1, :],
                                             ALU.subtract)
                made.then_inc(shift_step, 1)

            def statistics(b, t):
                dve.bn_aggr(mv[:, t, :], stats[:, t, :]).then_inc(mv_ready, 1)

            def normalise(b, t):
                dve.wait_ge(norm_step, NORM_STEPS * QTILES * b + 2 * t + 2)
                dve.tensor_scalar(z[:, t, :], y[:, t, :], mv[:, t, 0:1], rstd[:, t, 1:2],
                                  ALU.subtract, ALU.mult).then_inc(z_ready, 1)

            def items(b, slots):
                before, after = {}, {}
                flat = [x for slot in slots for x in slot]

                def stats_wait(t):
                    dve.wait_ge(stats_ready, QTILES * b + t + 1)

                for at, (n, it) in enumerate(flat):
                    if it[0] == "m":
                        for late in sorted(k for k in after if k >= at):
                            for what, args in [x for x in after[late] if x[0] is shift]:
                                what(b, *args)
                                after[late].remove((what, args))
                    for t in before.pop(at, []):
                        stats_wait(t)
                    item(b, n, it)
                    for what, args in after.pop(at, []):
                        what(b, *args)
                    if it[0] == "y":
                        before.setdefault(at + 1, []).append(it[1])
                        after.setdefault(at + 1, []).append((statistics, (it[1],)))
                        after.setdefault(at + NORM_LAG, []).append((normalise, (it[1],)))
                    if it[0] == "s" and it[2:] == (GROUP - 1, SMAX - 1):
                        last_max[it[1]] = n
                        for step in range(SHIFT_STEPS):
                            after.setdefault(at + 1 + step, []).append((shift, (it[1], step)))
                for at in sorted(after):
                    for t in before.get(at, []):
                        stats_wait(t)
                    for what, args in after[at]:
                        what(b, *args)

            last_max = {}
            items(0, [plan.prologue] + plan.unit0)
            with dve.Fori(0, BATCHES - 1) as b:
                items(b, [slot for slots in plan.body for slot in slots])
            items(BATCHES - 1, [slot for slots in plan.tail for slot in slots])
            items(BATCHES - 1, [plan.ending])

        @block.tensor
        def _(pe):
            pe.wait_ge(weights_loaded, 16 * WEIGHTS)
            pe.wait_ge(consts_made, CONSTS)

            def bank_free(b, n):
                before = n - BANKS
                if before >= 0:
                    pb = b
                else:
                    before = n + (NPIECES - 1 - n) // BANKS * BANKS
                    pb = b - 1
                count = sum(BY_DVE[i] == BY_DVE[before] for i in range(before + 1))
                if isinstance(pb, int) and pb < 0:
                    return
                if BY_DVE[before]:
                    pe.wait_ge(dve_took, DVE_PIECES * pb + count)
                else:
                    pe.wait_ge(act_took, ACT_PIECES * pb + count)

            def project(b):
                for n, (kind, h, c) in enumerate(PIECES):
                    bank, width = psum[:, n % BANKS, :], CHUNKS[c]
                    bank_free(b, n)
                    if n == 0:
                        pe.wait_ge(x_loaded, 16 * (b + 1))
                    if n == HALVES:
                        pe.wait_ge(ctx_loaded, 32 * (b + 1))
                    if n == TURNS:
                        pe.wait_ge(act_took, ACT_PIECES * b + HALVES)
                    if n == TURNS + HALVES:
                        pe.wait_ge(act_took, ACT_PIECES * b + TURNS)
                    if kind == "xt":
                        for t in range(QTILES):
                            mm = pe.transpose(bank[:, t * P:(t + 1) * P], x_in[:, t, h * P:(h + 1) * P], ident[:, :])
                    elif kind == "ct":
                        for i in range(0, width, P):
                            w = min(P, width - i)
                            mm = pe.transpose(bank[:, i:i + w], ctx_in[0:w, (c * BANK + i) // P, h * P:(h + 1) * P],
                                              ident[0:w, 0:w])
                    elif kind == "v":
                        for i in range(min(2, KTILES - h)):
                            w = P if h + i < FULL else REST
                            for k in range(HALVES):
                                mm = pe.matmul(bank[0:w, i * DIM:(i + 1) * DIM],
                                               ctxT[:, k, (h + i) * P:(h + i) * P + w], wv[:, k, :],
                                               start=(k == 0), stop=(k == HALVES - 1))
                    else:
                        w, src = (wk, ctxT) if kind == "k" else (wq, xT)
                        for k in range(HALVES):
                            mm = pe.matmul(bank[:, 0:width], w[:, k, h * P:(h + 1) * P],
                                           src[:, k, c * BANK:c * BANK + width],
                                           start=(k == 0), stop=(k == HALVES - 1))
                    mm.then_inc(piece_made, 1)

            project(0)
            with pe.Fori(1, BATCHES) as b:
                project(b)
            pe.wait_ge(act_took, ACT_PIECES * BATCHES)
            pe.wait_ge(dve_took, DVE_PIECES * BATCHES)
            pe.matmul(o_bank, zeros[0:PROD, 0:P], zeros[0:PROD, :], start=True, stop=True)

            def item(b, n, it):
                at = LOOP_ITEMS * b + n
                bank = ring[n % RING]
                if not (isinstance(b, int) and at < RING):
                    pe.wait_ge(item_taken, at - RING + 1)
                if it[0] == "s":
                    _, r, h, j = it
                    bb, g = vitem(b, r)
                    if h == 0 and j == 0:
                        pe.wait_ge(kq_loaded[g], 16 * KQ_DMAS * (bb + 1))
                    if j < SMAX - 1:
                        t, c = divmod(j, len(CHUNKS) - 1)
                        mm = pe.matmul(bank, qrys[g][0:PROD, h, t * P:(t + 1) * P],
                                       keys[g][0:PROD, h, c * BANK:(c + 1) * BANK], start=True, stop=True)
                    else:
                        for t in range(QTILES):
                            mm = pe.matmul(bank[:, t * REST:(t + 1) * REST], qrys[g][0:PROD, h, t * P:(t + 1) * P],
                                           keys[g][0:PROD, h, KEYS - REST:KEYS], start=True, stop=True)
                elif it[0] == "m":
                    r = it[1]
                    pe.wait_ge(shift_step, SHIFT_STEPS * (GROUPS * b + r + 1))
                    mm = pe.transpose(bank.bitcast(BF16)[:, 0:P], negpad[r % 2][:, :], identb[:, :])
                elif it[0] == "o":
                    t = it[1]
                    pe.wait_ge(o_copied, GROUPS * (b + 1))
                    for g in range(GROUPS):
                        mm = pe.transpose(bank[:, g * P:(g + 1) * P], o_out[:, g, t * P:(t + 1) * P], ident[:, :])
                elif it[0] == "n":
                    pe.wait_ge(item_taken, LOOP_ITEMS * b + ending_at[("o", 2 * it[1] + 1)] + 1)
                    for i in range(2):
                        src = o_norm[:, 2 * it[1] + i, :, :].rearrange("p h d -> p (h d)")
                        for h in range(HALVES):
                            mm = pe.transpose(bank[:, (i * HALVES + h) * P:(i * HALVES + h + 1) * P],
                                              src[:, h * P:(h + 1) * P], ident[:, :])
                else:
                    t = it[1]
                    pe.wait_ge(item_taken, LOOP_ITEMS * b + ending_at[("n", t // 2)] + 1)
                    for h in range(HALVES):
                        mm = pe.matmul(bank[:, 0:DIM], o_normT[:, t, h, :], wo[:, h, :],
                                       start=(h == 0), stop=(h == HALVES - 1))
                mm.then_inc(item_made, 1)

            def scores(b, r, kt, h):
                p, i = divmod(h, 2)
                u = GROUPS * b + r
                s = KTILES * u + kt
                bb, g = vitem(b, r)
                if i == 0 and not (isinstance(u, int) and s == 0):
                    pe.wait_ge(probs_ready, 2 * s + p - 1)
                if kt == 0 and h == 0:
                    pe.wait_ge(ones_made, GROUPS)
                    pe.wait_ge(shift_placed[g], 16 * PARTS * (bb + 1))
                w = P if kt < FULL else REST
                mm = pe.matmul(s_bank[p][i][0:w, :], keys[g][:, 2 * p + i, kt * P:kt * P + w],
                               qrys[g][:, 2 * p + i, :], start=True, stop=True)
                if i == 1:
                    mm.then_inc(scores_ready, 1)

            def times_v(b, r, kt):
                u = GROUPS * b + r
                s = KTILES * u + kt
                bb, g = vitem(b, r)
                pe.wait_ge(probs_ready, 2 * s + 2)
                if kt == 0:
                    pe.wait_ge(v_loaded[g], 16 * V_DMAS * (bb + 1))
                    pe.wait_ge(o_copied, u)
                w = P if kt < FULL else REST
                buf = (KTILES * r + kt) % PBUFS
                for h in range(GROUP):
                    mm = pe.matmul(o_bank[32 * h:32 * h + VW, :], vals[g][0:w, kt, h, :],
                                   probs[0:w, buf, h * BANK:(h + 1) * BANK],
                                   start=(kt == 0), stop=(kt == KTILES - 1))
                mm.then_inc(pv_done, 1)

            def unit(b, r, slots, first=False):
                for kt in range(KTILES):
                    for h in range(GROUP):
                        scores(b, r, kt, h)
                        for n, it in slots[GROUP * kt + h]:
                            item(b, n, it)
                    if kt:
                        times_v(b, r, kt - 1)
                    elif not first:
                        times_v(b, r - 1, KTILES - 1)

            ending_at = {it: n for slots in plan.body for slot in slots for n, it in slot}
            for n, it in plan.prologue:
                item(0, n, it)
            unit(0, 0, plan.unit0, first=True)
            with pe.Fori(0, BATCHES - 1) as b:
                for r in range(1, GROUPS + 1):
                    unit(b, r, plan.body[r - 1])
            for r in range(1, GROUPS):
                unit(BATCHES - 1, r, plan.tail[r - 1])
            times_v(BATCHES - 1, GROUPS - 1, KTILES - 1)
            ending_at = {it: n for n, it in plan.ending}
            for n, it in plan.ending:
                item(BATCHES - 1, n, it)


_INS = ["x", "ctx_1024", "L0_xattn_Wq", "L0_xattn_bq", "L0_xattn_Wk", "L0_xattn_bk", "L0_xattn_Wv", "L0_xattn_bv",
        "L0_xattn_Wo", "L0_xattn_bo", "L0_xattn_ln_g", "L0_xattn_ln_b"]


def kernel(**inputs):
    import numpy as np
    import concourse.bacc as bacc
    from concourse.bass_utils import run_bass_kernel_spmd

    nc = bacc.Bacc("TRN2", target_bir_lowering=False, num_devices=1)
    arrays, args = {}, []
    for name in _INS:
        a = np.ascontiguousarray(inputs[name])
        arrays[f"in_{name}"] = a
        args.append(nc.dram_tensor(f"in_{name}", a.shape, mybir.dt.from_np(a.dtype), kind="ExternalInput").ap())
    out = nc.dram_tensor("out_x", (BATCHES, QUERIES, DIM), F32, kind="ExternalOutput").ap()
    xattn_kernel(nc, *args, out)
    r = run_bass_kernel_spmd(nc, [arrays], core_ids=[0])
    return r.results[0]["out_x"]
```

```python
from contextlib import ExitStack

import concourse.bass as bass
from concourse import mybir

F32 = mybir.dt.float32
F32R = mybir.dt.float32r
BF16 = mybir.dt.bfloat16
ALU = mybir.AluOpType
ACT = mybir.ActivationFunctionType
AX = mybir.AxisListType

P = 128
BANK = 512
BATCHES, QUERIES, DIM = 8, 512, 256
KEYS = 1601
HEADS, HD = 16, 16
LN_EPS = 1e-5

HALVES = DIM // P
GROUP = 4
GROUPS = HEADS // GROUP
QTILES = QUERIES // P
FULL = KEYS // P
REST = KEYS - FULL * P
KTILES = FULL + 1
CHUNKS = [BANK] * (KEYS // BANK) + [KEYS % BANK]
assert CHUNKS[-1] == REST and QUERIES == BANK
PARTS = 3
PROD = 6 * HD
ROWS = PROD + PARTS
KPITCH = KEYS + 7
CPITCH = KEYS + 1
VW = HD + 1
SCALE = 1.0 / HD ** 0.5

KWIDTH = 2 * -(-CPITCH // (2 * len(CHUNKS)))
KCHUNKS = [(i, min(KWIDTH, KEYS - i)) for i in range(0, KEYS, KWIDTH)]
assert len(KCHUNKS) == len(CHUNKS) and KWIDTH <= BANK
CTX_LOADS = [(0, 2 * QTILES), (2 * QTILES, FULL)]
PIECES = ([("xt", h, 0) for h in range(HALVES)]
          + [("ct", h, c) for c in range(len(CHUNKS)) for h in range(HALVES)]
          + [("q", m, 0) for m in range(HALVES)]
          + [("v", t, 0) for t in range(0, KTILES, 2)]
          + [("k", m, c) for m in range(HALVES) for c in range(len(CHUNKS))])
NPIECES = len(PIECES)
TURNS = sum(p[0] in ("xt", "ct") for p in PIECES)
BY_DVE = [p[0] == "v" for p in PIECES]
ACT_PIECES, DVE_PIECES = NPIECES - sum(BY_DVE), sum(BY_DVE)
BANKS = 8
SPLITS = 3
EARLY_FROM = 2
EARLY_TILES = QTILES // 2
EARLY = GROUP * EARLY_TILES
EARLY_CHUNKS = len(CHUNKS) - 1
assert (BATCHES - EARLY_FROM) == 2 * EARLY_CHUNKS
EARLY_BEFORE = (1, 1, 2, 3, 4, 5, 5, 6)
EARLY_AT = [[n for n, before in enumerate(EARLY_BEFORE) if piece == NPIECES - HALVES * len(CHUNKS) + before]
            for piece in range(NPIECES)]
HI, LO = 0, 1
PAIRS = [(HI, HI), (LO, HI), (HI, LO)]

RING = 3
SMAX = QTILES * (len(CHUNKS) - 1) + 1
PERIOD = GROUP * SMAX + 1
LEAD = [20, 13, 16, 18]
TURN_AT = 7
FIRST_LEAD, FIRST_TURN_AT = 8, 2
PBUFS = 2
NORM_LAG = 6
SHIFT_STEPS = 5


def period(r):
    items = [("s", r, h, j) for h in range(GROUP) for j in range(SMAX)]
    return items[:TURN_AT] + [("m", r - 1)] + items[TURN_AT:]


ENDING = ([(7 + 2 * t, ("o", t)) for t in range(QTILES)]
          + [(16 + 2 * t, ("n", t // 2)) for t in range(0, QTILES, 2)]
          + [(23 + 4 * t, ("y", t)) for t in range(QTILES)])
LOOP_ITEMS = GROUPS * PERIOD + len(ENDING)
assert LOOP_ITEMS % RING == 0 and (GROUPS * KTILES) % PBUFS == 0


def spread(items, ending, over=GROUP * KTILES):
    slots = [[] for _ in range(GROUP * KTILES)]
    for n, it in enumerate(items):
        slots[n * over // len(items)].append(it)
    for quarter, it in ending:
        slots[quarter].insert(0, it)
    return slots


def columns(kind, c):
    return KCHUNKS[c] if kind == "k" else (c * BANK, CHUNKS[c])


def is_last_maxima(it):
    return it[0] == "s" and it[2:] == (GROUP - 1, SMAX - 1)


def is_first(b):
    return isinstance(b, int) and b == 0


class Plan:

    def __init__(self):
        ahead = period(1)[:FIRST_LEAD]
        ahead.insert(FIRST_TURN_AT, ahead.pop(ahead.index(("m", 0))))
        first = [("s", 0, h, SMAX - 1) for h in range(GROUP)] + ahead
        self.count = EARLY * (BATCHES - EARLY_FROM)
        self.prologue = self.numbered([first])[0]
        self.unit0 = self.unit(0, [], lead=FIRST_LEAD)
        self.loop_start = self.count
        self.body = [self.unit(r, ENDING if r == GROUPS else []) for r in range(1, GROUPS + 1)]
        assert self.count == self.loop_start + LOOP_ITEMS
        self.count = self.loop_start
        self.tail = [self.unit(1, []), self.unit(2, [], last=True), self.unit(3, [], none=True)]
        self.ending = self.numbered([[it for _, it in ENDING]])[0]
        self.turn_of = {}
        for b, units in ((0, [[self.prologue], self.unit0]), (None, self.body), (BATCHES - 1, self.tail)):
            self.turn_of |= {(b, it[1]): n for slots in units for slot in slots for n, it in slot if it[0] == "m"}
        at = {it: n for slots in self.body for slot in slots for n, it in slot}
        self.turned = at[("o", QTILES - 1)] - LOOP_ITEMS

    def numbered(self, slots):
        out = []
        for slot in slots:
            out.append([(self.count + n, it) for n, it in enumerate(slot)])
            self.count += len(slot)
        return out

    def unit(self, r, ending, lead=None, last=False, none=False):
        lead = LEAD[r % GROUPS] if lead is None else lead
        items = period(r + 1)[lead:] + period(r + 2)[:LEAD[(r + 1) % GROUPS]]
        if last:
            over = GROUP * (KTILES - 3)
            slots = spread(period(r + 1)[lead:], ending, over)
            slots[over + 3].append(("m", r + 1))
            return self.numbered(slots)
        return self.numbered(spread([] if none else items, ending))


def xattn_kernel(nc, x, ctx, Wq, bq, Wk, bk, Wv, bv, Wo, bo, ln_g, ln_b, out):
    plan = Plan()
    kparts = nc.dram_tensor("kparts", [BATCHES, HEADS, PARTS * HD, KEYS], BF16, kind="Internal").ap()
    qparts = nc.dram_tensor("qparts", [BATCHES, HEADS, PARTS * HD, QUERIES], BF16, kind="Internal").ap()
    vunits = nc.dram_tensor("vunits", [BATCHES, GROUPS, P, KTILES * GROUP * VW], F32, kind="Internal").ap()

    with ExitStack() as stack:
        def sb(name, shape, dt):
            return stack.enter_context(nc.sbuf_tensor(name, shape, dt))

        def sem(name):
            return stack.enter_context(nc.semaphore(name))

        ident = sb("ident", [P, P], F32)
        identb = sb("identb", [P, P], BF16)
        zeros = sb("zeros", [P, BANK], BF16)
        wo = sb("wo", [P, HALVES, DIM], F32)
        wparts = [sb(f"wparts{n}", [P, 3, HALVES, DIM], F32R) for n in (HI, LO)]
        bq_col, bk_col = (sb(n, [P, HALVES], F32) for n in ("bq_col", "bk_col"))
        bv_row, bo_row, g_row, b_row = (sb(n, [P, DIM], F32) for n in ("bv_row", "bo_row", "g_row", "b_row"))
        minus_half = sb("minus_half", [P, 1], F32)
        eps = sb("eps", [P, 1], F32)
        probs = sb("probs", [P, PBUFS, GROUP * BANK], F32)
        flat = probs[:, :, :].rearrange("p a b -> p (a b)")
        ctx_in = flat[:, 0:KTILES * DIM].rearrange("p (t d) -> p t d", t=KTILES)
        x_in = sb("x_in", [P, QTILES, DIM], F32)
        ctxT = [sb(f"ctxT{n}", [P, HALVES, CPITCH], F32R) for n in (HI, LO)]
        xT = [sb(f"xT{n}", [P, HALVES, QUERIES], F32R) for n in (HI, LO)]
        kf = sb("kf", [P, HALVES, KEYS], F32)
        qf = sb("qf", [P, HALVES, QUERIES], F32)
        left, pool_left = (sb(n, [P, KEYS], F32) for n in ("left", "pool_left"))
        v_out = sb("v_out", [P, GROUPS, KTILES, GROUP, VW], F32)
        keys_all = sb("keys_all", [P, GROUPS, GROUP * KPITCH], BF16)
        keys = [keys_all[0:ROWS, g, :].rearrange("p (h k) -> p h k", h=GROUP) for g in range(GROUPS)]
        qrys = [sb(f"qrys{g}", [ROWS, GROUP, QUERIES], BF16) for g in range(GROUPS)]
        vals = [sb(f"vals{g}", [P, KTILES, GROUP, VW], F32) for g in range(GROUPS)]
        mx = [sb(f"mx{n}", [P, GROUP, QTILES, len(CHUNKS)], F32) for n in range(2)]
        neg = [sb(f"neg{n}", [P, GROUP * QTILES], F32) for n in range(2)]
        negleft = [sb(f"negleft{n}", [P, GROUP * QTILES], F32) for n in range(2)]
        negpad = [sb(f"negpad{n}", [P, P], BF16) for n in range(2)]
        negparts = [t[:, 0:PARTS * GROUP * QTILES].rearrange("p (i n) -> p i n", i=PARTS) for t in negpad]
        negT = [sb(f"negT{n}", [PARTS * GROUP * QTILES, P], BF16) for n in range(2)]
        keys_later = keys_all[:, 2:GROUPS, :].rearrange("p g n -> p (g n)")
        kp_size, qp_size = HALVES * PARTS * KEYS, HALVES * PARTS * QUERIES
        assert kp_size + qp_size <= 2 * GROUP * KPITCH
        kp = keys_later[:, 0:kp_size].rearrange("p (m i k) -> p m i k", m=HALVES, i=PARTS)
        qp = keys_later[:, kp_size:kp_size + qp_size].rearrange("p (m i k) -> p m i k", m=HALVES, i=PARTS)

        def over(tensor, start, *dims):
            n = 1
            for d in dims:
                n *= d
            names = "abc"[:len(dims)]
            return tensor[:, start:start + n].rearrange(
                f"p ({' '.join(names)}) -> p {' '.join(names)}", **dict(zip(names, dims)))

        kf_flat = kf[:, :, :].rearrange("p h k -> p (h k)")
        w_in = over(kf_flat, 0, 3, HALVES, DIM)
        o_out = over(v_out[:, :, :, :, :].rearrange("p g t h w -> p (g t h w)"), 0, GROUPS, QUERIES)
        rden = sb("rden", [P, QTILES, HEADS], F32)
        o_norm = over(kf_flat, 0, QTILES, HEADS, HD)
        o_normT = over(kf_flat, QTILES * DIM, QTILES, HALVES, P)
        resid = sb("resid", [P, QTILES, DIM], F32)
        y = over(kf_flat, 2 * QTILES * DIM, QTILES, DIM)
        stats = sb("stats", [P, QTILES, 6], F32)
        mv = sb("mv", [P, QTILES, 2], F32)
        rstd = sb("rstd", [P, QTILES, 2], F32)
        z = over(left, 0, QTILES, DIM)

        psum = stack.enter_context(nc.psum_tensor("psum", [P, BANKS, BANK], F32))
        s_bank = [[psum[:, 2 * p + n, :] for n in range(2)] for p in range(2)]
        s_pair = [psum[:, 2 * p:2 * p + 2, :].rearrange("p a b -> p (a b)") for p in range(2)]
        ring = [psum[:, 4 + n, :] for n in range(RING)]
        o_bank = psum[:, BANKS - 1, :]

        weights_loaded = sem("weights_loaded")
        wo_loaded = sem("wo_loaded")
        columns_loaded = sem("columns_loaded")
        rows_loaded = sem("rows_loaded")
        ident_cleared = sem("ident_cleared")
        ident_made = sem("ident_made")
        consts_made = sem("consts_made")
        ones_made = sem("ones_made")
        x_loaded = sem("x_loaded")
        ctx_loaded = [sem(f"ctx_loaded{n}") for n in range(len(CTX_LOADS) + 1)]
        piece_made = sem("piece_made")
        act_took = sem("act_took")
        dve_took = sem("dve_took")
        weights_hi = sem("weights_hi")
        weights_lo = sem("weights_lo")
        lo_took = sem("lo_took")
        k_split = [sem(f"k_split{m}") for m in range(HALVES)]
        q_split = sem("q_split")
        q_written = sem("q_written")
        v_written = sem("v_written")
        k_written = [sem(f"k_written{m}") for m in range(HALVES)]
        v_ones = sem("v_ones")
        kq_loaded = [sem(f"kq_loaded{g}") for g in range(GROUPS)]
        v_loaded = [sem(f"v_loaded{g}") for g in range(GROUPS)]
        item_made = sem("item_made")
        item_taken = sem("item_taken")
        shift_step = sem("shift_step")
        shift_placed = [sem(f"shift_placed{g}") for g in range(GROUPS)]
        scores_ready = sem("scores_ready")
        probs_ready = sem("probs_ready")
        pv_done = sem("pv_done")
        o_copied = sem("o_copied")
        rden_ready = sem("rden_ready")
        y_ready = sem("y_ready")
        stats_ready = sem("stats_ready")
        mv_ready = sem("mv_ready")
        resid_loaded = sem("resid_loaded")
        resid_ready = sem("resid_ready")
        norm_step = sem("norm_step")
        z_ready = sem("z_ready")
        out_written = sem("out_written")
        last_scaled = sem("last_scaled")
        last_ready = sem("last_ready")
        last_written = sem("last_written")
        KQ_DMAS, V_DMAS = 9, 1
        ROWS_N = 4
        NORM_STEPS = 4
        CONSTS = 1 + 2 + 1 + 2

        def early_bank(n):
            return (NPIECES - 2 + n % 2) % BANKS

        def vitem(b, r):
            return b + r // GROUPS, r % GROUPS

        block = stack.enter_context(nc.Block())

        @block.sync
        def _(sp):
            def load_weights():
                for n, w in enumerate((Wq, Wk, Wv)):
                    sp.dma_start(w_in[:, n], w.rearrange("(h p) n -> p h n", p=P)).then_inc(weights_loaded, 16)

            def load_inputs(b):
                sp.dma_start(x_in[:, :, :], x[b].rearrange("(t p) d -> p t d", p=P)).then_inc(x_loaded, 16)
                if is_first(b):
                    load_weights()
                for n, (first, end) in enumerate(CTX_LOADS):
                    sp.dma_start(ctx_in[:, first:end, :],
                                 ctx[b, first * P:end * P, :].rearrange("(t p) d -> p t d", p=P)
                                 ).then_inc(ctx_loaded[n], 16)
                sp.dma_start(ctx_in[0:REST, FULL, :], ctx[b, FULL * P:KEYS, :]).then_inc(ctx_loaded[-1], 16)

            def store_parts(b, m, src, dst, written):
                for i in range(PARTS):
                    sp.dma_start(dst[b, m * HEADS // HALVES:(m + 1) * HEADS // HALVES, i * HD:(i + 1) * HD, :],
                                 src[:, m, i, :]).then_inc(written, 16)

            def store_q(b):
                for m in range(HALVES):
                    sp.wait_ge(q_split, SPLITS * (HALVES * b + m + 1))
                    store_parts(b, m, qp, qparts, q_written)

            def store_k(b):
                for m in range(HALVES):
                    sp.wait_ge(k_split[m], SPLITS * (b + 1))
                    store_parts(b, m, kp, kparts, k_written[m])

            def store_v(b):
                sp.wait_ge(dve_took, DVE_PIECES * (b + 1))
                sp.dma_start(vunits[b].rearrange("g p n -> p g n"),
                             v_out[:, :, :, :, :].rearrange("p g t h w -> p g (t h w)")).then_inc(v_written, 16)

            def turned(b):
                sp.wait_ge(piece_made, NPIECES * b + TURNS)

            load_inputs(0)
            sp.dma_start(wo[:, :, :], Wo.rearrange("(h p) n -> p h n", p=P)).then_inc(wo_loaded, 16)
            with nc.allow_non_contiguous_dma("two columns of biases"):
                for t, v in ((bq_col, bq), (bk_col, bk)):
                    sp.dma_start(t[:, :], v.rearrange("(h p) -> p h", p=P)).then_inc(columns_loaded, 16)

            turned(0)
            load_inputs(1)
            store_v(0)
            store_q(0)

            def load_and_store(b):
                turned(b)
                load_inputs(b + 1)
                store_k(b - 1)
                store_v(b)
                store_q(b)

            def load_kq(b, g):
                heads = slice(g * GROUP, (g + 1) * GROUP)
                row = 0
                for n in (3, 2, 1):
                    sp.dma_start(keys[g][row:row + n * HD, :, 0:KEYS],
                                 kparts[b, heads, 0:n * HD, :].rearrange("h r k -> r h k")
                                 ).then_inc(kq_loaded[g], 16)
                    for _ in range(n):
                        i = PARTS - n
                        sp.dma_start(qrys[g][row:row + HD, :, :],
                                     qparts[b, heads, i * HD:(i + 1) * HD, :].rearrange("h r k -> r h k")
                                     ).then_inc(kq_loaded[g], 16)
                        row += HD

            def load_v(b, g):
                sp.dma_start(vals[g][:, :, :, :].rearrange("p t h w -> p (t h w)"), vunits[b, g]
                             ).then_inc(v_loaded[g], 16)

            def place_shift(b, r):
                bb, g = vitem(b, r)
                sp.wait_ge(item_taken, LOOP_ITEMS * b + plan.turn_of[b if isinstance(b, int) else None, r] + 1)
                n = GROUP * QTILES
                for i in range(PARTS):
                    sp.dma_start(qrys[g][PROD + i:PROD + i + 1, :, :].rearrange("o h (t j) -> o (h t) j", j=P),
                                 negT[r % 2][i * n:(i + 1) * n, :]).then_inc(shift_placed[g], 16)

            def parts_stored(batches):
                sp.wait_ge(q_written, 16 * HALVES * PARTS * batches)
                sp.wait_ge(v_written, 16 * batches)
                for m in range(HALVES):
                    sp.wait_ge(k_written[m], 16 * PARTS * batches)

            load_and_store(1)
            parts_stored(1)
            load_kq(0, 0)
            with sp.Fori(EARLY_FROM, BATCHES - 1) as b:
                load_and_store(b)
            load_kq(0, 1)
            store_k(BATCHES - 2)
            for g in range(GROUPS):
                load_v(0, g)
            store_v(BATCHES - 1)
            store_q(BATCHES - 1)
            place_shift(0, 0)
            store_k(BATCHES - 1)
            parts_stored(BATCHES)
            load_kq(0, 2)
            load_kq(0, 3)
            place_shift(0, 1)
            with sp.Fori(0, BATCHES - 1) as b:
                for r in range(1, GROUPS + 1):
                    sp.wait_ge(pv_done, KTILES * (GROUPS * b + r))
                    load_kq(b + 1, r - 1)
                    load_v(b + 1, r - 1)
                    place_shift(b, r + 1)
            b = BATCHES - 1
            for r in range(2, GROUPS):
                place_shift(b, r)
            for t in range(QTILES):
                sp.wait_ge(last_ready, t + 1)
                sp.dma_start(out[b, t * P:(t + 1) * P, :], z[:, t, :]).then_inc(last_written, 16)
            sp.wait_ge(last_written, 16 * QTILES)

        @block.gpsimd
        def _(pool):
            pool.memset(ident[:, :], 0.0).then_inc(ident_cleared, 1)
            pool.memset(minus_half[:, :], -0.5).then_inc(ident_cleared, 1)
            pool.memset(eps[:, :], LN_EPS).then_inc(ident_cleared, 1)
            pool.wait_ge(ident_cleared, 3)
            pool.affine_select(out=ident[:, :], in_=ident[:, :], compare_op=ALU.not_equal, fill=1.0, base=0,
                               pattern=[[-1, P]], channel_multiplier=1).then_inc(ident_made, 1)

            def key_ones(g):
                pool.memset(keys[g][PROD:ROWS, :, :], 1.0).then_inc(ones_made, 1)
                pool.wait_ge(ones_made, g + 1)

            for t, v in ((bv_row, bv), (bo_row, bo), (g_row, ln_g), (b_row, ln_b)):
                pool.dma_start(t[:, :], v.partition_broadcast(P)).then_inc(rows_loaded, 16)
            pool.wait_ge(ident_made, 1)
            key_ones(0)
            key_ones(1)
            pool.wait_ge(rows_loaded, 16 * ROWS_N)
            pool.wait_ge(consts_made, CONSTS)

            def split(base, done, full, parts):
                left, zero = pool_left[:, 0:full.shape[-1]], zeros[:, 0:1].to_broadcast([P, full.shape[-1]])
                pool.tensor_tensor(left, full, parts[:, 0, :], ALU.subtract).then_inc(done, 1)
                pool.wait_ge(done, base + 1)
                pool.tensor_tensor(parts[:, 1, :], left, zero, ALU.add).then_inc(done, 1)
                pool.wait_ge(done, base + 2)
                pool.tensor_tensor(parts[:, 2, :], left, parts[:, 1, :], ALU.subtract).then_inc(done, 1)
                pool.wait_ge(done, base + 3)

            def split_q(b):
                for m in range(HALVES):
                    pool.wait_ge(act_took, ACT_PIECES * b + TURNS + m + 1)
                    split(SPLITS * (HALVES * b + m), q_split, qf[:, m, :], qp[:, m])

            def split_k(b, m):
                pool.wait_ge(act_took, ACT_PIECES * b + TURNS + HALVES + (m + 1) * len(CHUNKS))
                split(SPLITS * b, k_split[m], kf[:, m, :], kp[:, m])

            split_q(0)
            with pool.Fori(1, BATCHES) as b:
                split_k(b - 1, 1)
                split_q(b)
            for m in range(HALVES):
                split_k(BATCHES - 1, m)
            pool.wait_ge(q_written, 16 * HALVES * PARTS * BATCHES)
            for m in range(HALVES):
                pool.wait_ge(k_written[m], 16 * PARTS * BATCHES)
            key_ones(2)
            key_ones(3)

            def residual(b):
                pool.dma_start(resid[:, :, :], x[b].rearrange("(t p) d -> p t d", p=P)).then_inc(resid_loaded, 16)
                pool.wait_ge(resid_loaded, 16 * (b + 1))
                for t in range(QTILES):
                    pool.tensor_tensor(resid[:, t, :], resid[:, t, :], bo_row[:, :], ALU.add
                                       ).then_inc(resid_ready, 1)

            def root(b):
                for t in range(QTILES):
                    base = NORM_STEPS * QTILES * b + 2 * t
                    pool.wait_ge(mv_ready, QTILES * b + t + 1)
                    pool.tensor_tensor(rstd[:, t, 0:1], mv[:, t, 1:2], eps[:, :], ALU.add).then_inc(norm_step, 1)
                    pool.wait_ge(norm_step, base + 1)
                    pool.tensor_tensor(rstd[:, t, 1:2], rstd[:, t, 0:1], minus_half[:, :], ALU.pow
                                       ).then_inc(norm_step, 1)

            def scale_and_store(b):
                for t in range(QTILES):
                    base = NORM_STEPS * QTILES * b + 2 * QTILES + 2 * t
                    pool.wait_ge(z_ready, QTILES * b + t + 1)
                    pool.tensor_tensor(z[:, t, :], z[:, t, :], g_row[:, :], ALU.mult).then_inc(norm_step, 1)
                    pool.wait_ge(norm_step, base + 1)
                    pool.tensor_tensor(z[:, t, :], z[:, t, :], b_row[:, :], ALU.add).then_inc(norm_step, 1)
                    pool.wait_ge(norm_step, base + 2)
                    pool.dma_start(out[b, t * P:(t + 1) * P, :], z[:, t, :]).then_inc(out_written, 16)

            residual(0)
            with pool.Fori(0, BATCHES - 1) as b:
                root(b)
                scale_and_store(b)
                pool.wait_ge(out_written, 16 * QTILES * (b + 1))
                residual(b + 1)
            root(BATCHES - 1)
            pool.wait_ge(out_written, 16 * QTILES * (BATCHES - 1))

        @block.scalar
        def _(act):
            act.wait_ge(weights_loaded, 16 * 3)
            act.activation(wparts[HI][:, :, :, :], w_in, ACT.Copy).then_inc(weights_hi, 1)
            act.wait_ge(weights_lo, 1)

            def take_pieces(b):
                for n, (kind, h, c) in enumerate(PIECES):
                    if BY_DVE[n]:
                        continue
                    first, width = columns(kind, c)
                    src, cols = psum[:, n % BANKS, 0:width], slice(first, first + width)
                    act.wait_ge(piece_made, NPIECES * b + n + 1)
                    if kind in ("xt", "ct"):
                        act.activation((xT if kind == "xt" else ctxT)[HI][:, h, cols], src, ACT.Copy
                                       ).then_inc(act_took, 1)
                        continue
                    full, parts, bias = (qf, qp, bq_col) if kind == "q" else (kf, kp, bk_col)
                    if is_first(b):
                        act.wait_ge(columns_loaded, 16 * 2)
                    elif kind == "q":
                        act.wait_ge(q_split, SPLITS * HALVES * b)
                        act.wait_ge(q_written, 16 * HALVES * PARTS * b)
                    else:
                        act.wait_ge(k_split[h], SPLITS * b)
                        act.wait_ge(k_written[h], 16 * PARTS * b)
                    act.activation(full[:, h, cols], src, ACT.Identity, bias=bias[:, h:h + 1])
                    act.activation(parts[:, h, 0, cols], src, ACT.Identity, bias=bias[:, h:h + 1]
                                   ).then_inc(act_took, 1)

            take_pieces(0)
            with act.Fori(1, BATCHES) as b:
                take_pieces(b)

            def unit(b, r, first=False):
                u = GROUPS * b + r
                for kt in range(KTILES):
                    s = KTILES * u + kt
                    rows = P if kt < FULL else REST
                    for p in range(2):
                        act.wait_ge(scores_ready, 2 * s + p + 1)
                        if not first or kt >= PBUFS:
                            act.wait_ge(pv_done, s - PBUFS + 1)
                        buf = (KTILES * r + kt) % PBUFS
                        act.activation(probs[0:rows, buf, p * 2 * BANK:(p + 1) * 2 * BANK],
                                       s_pair[p][0:rows, :], ACT.Exp, scale=SCALE).then_inc(probs_ready, 1)
                    if kt == 0 and not first:
                        copy_out(b, r - 1)

            def copy_out(b, r):
                act.wait_ge(pv_done, KTILES * (GROUPS * b + r + 1))
                if r == 0:
                    act.wait_ge(item_made, LOOP_ITEMS * b + plan.turned + 1)
                act.activation(o_out[:, r, :], o_bank, ACT.Copy).then_inc(o_copied, 1)

            unit(0, 0, first=True)
            with act.Fori(0, BATCHES - 1) as b:
                for r in range(1, GROUPS + 1):
                    unit(b, r)
            for r in range(1, GROUPS):
                unit(BATCHES - 1, r)
            copy_out(BATCHES - 1, GROUPS - 1)

        @block.vector
        def _(dve):
            dve.memset(zeros[:, :], 0.0).then_inc(consts_made, 1)
            for t in ctxT:
                dve.memset(t[:, :, KEYS:CPITCH].bitcast(F32), 0.0).then_inc(consts_made, 1)
            for t in negpad:
                dve.memset(t[:, :], 0.0).then_inc(consts_made, 1)
            dve.wait_ge(ident_made, 1)
            dve.tensor_copy(identb[:, :], ident[:, :]).then_inc(consts_made, 1)
            dve.memset(v_out[:, :, :, :, :], 1.0).then_inc(v_ones, 1)

            dve.wait_ge(weights_hi, 1)
            dve.tensor_tensor(wparts[LO][:, :, :, :], w_in, wparts[HI][:, :, :, :].bitcast(F32), ALU.subtract
                              ).then_inc(weights_lo, 1)

            def split_k(b):
                dve.wait_ge(act_took, ACT_PIECES * b + TURNS + HALVES + len(CHUNKS))
                dve.wait_ge(dve_took, DVE_PIECES * (b + 1))
                dve.tensor_tensor(left[:, :], kf[:, 0, :], kp[:, 0, 0, :], ALU.subtract).then_inc(k_split[0], 1)
                dve.wait_ge(k_split[0], SPLITS * b + 1)
                dve.tensor_copy(kp[:, 0, 1, :], left[:, :]).then_inc(k_split[0], 1)
                dve.wait_ge(k_split[0], SPLITS * b + 2)
                dve.tensor_tensor(kp[:, 0, 2, :], left[:, :], kp[:, 0, 1, :], ALU.subtract).then_inc(k_split[0], 1)

            def take_and_split(b):
                for n, (kind, h, c) in enumerate(PIECES[:TURNS]):
                    parts, cols = xT if kind == "xt" else ctxT, slice(c * BANK, c * BANK + CHUNKS[c])
                    dve.wait_ge(act_took, ACT_PIECES * b + n + 1)
                    dve.tensor_tensor(parts[LO][:, h, cols], psum[:, n % BANKS, 0:CHUNKS[c]],
                                      parts[HI][:, h, cols].bitcast(F32), ALU.subtract).then_inc(lo_took, 1)
                if is_first(b):
                    dve.wait_ge(rows_loaded, 16 * ROWS_N)
                    dve.wait_ge(v_ones, 1)
                else:
                    split_k(b - 1)
                    dve.wait_ge(v_written, 16 * b)
                for n, (kind, t, _c) in enumerate(PIECES):
                    if not BY_DVE[n]:
                        continue
                    dve.wait_ge(piece_made, NPIECES * b + n + 1)
                    last = None
                    both = min(2, KTILES - t)
                    for i in range(both):
                        rows = P if t + i < FULL else REST
                        last = dve.tensor_tensor(
                            v_out[0:rows, :, t + i, :, 0:HD],
                            psum[0:rows, n % BANKS, i * DIM:(i + 1) * DIM].rearrange(
                                "p (g h d) -> p g h d", g=GROUPS, h=GROUP),
                            bv_row[0:rows, :].rearrange("p (g h d) -> p g h d", g=GROUPS, h=GROUP), ALU.add)
                    last.then_inc(dve_took, 1)

            def early_maxima(c, tiles):
                for n in range(EARLY):
                    h, i = divmod(n, EARLY_TILES)
                    dve.wait_ge(item_made, EARLY * (2 * c + tiles) + n + 1)
                    dve.tensor_reduce(mx[0][:, h, EARLY_TILES * tiles + i, bass.ds(c, 1)],
                                      psum[:, early_bank(n), :], AX.X, ALU.max).then_inc(item_taken, 1)

            for b in range(EARLY_FROM):
                take_and_split(b)
            with dve.Fori(0, EARLY_CHUNKS) as c:
                with dve.Fori(0, 2) as tiles:
                    take_and_split(EARLY_FROM + 2 * c + tiles)
                    early_maxima(c, tiles)

            def item(b, n, it):
                at = LOOP_ITEMS * b + n
                bank = ring[n % RING]
                dve.wait_ge(item_made, at + 1)
                if it[0] == "s":
                    _, r, h, j = it
                    if j < SMAX - 1:
                        t, c = divmod(j, len(CHUNKS) - 1)
                        dve.tensor_reduce(mx[r % 2][:, h, t, c:c + 1], bank, AX.X, ALU.max
                                          ).then_inc(item_taken, 1)
                    else:
                        dve.tensor_reduce(mx[r % 2][:, h, :, len(CHUNKS) - 1],
                                          bank[:, 0:QTILES * REST].rearrange("p (t k) -> p t k", t=QTILES),
                                          AX.X, ALU.max).then_inc(item_taken, 1)
                elif it[0] == "m":
                    r = it[1]
                    bb, g = vitem(b, r - 2)
                    if not (isinstance(bb, int) and bb < 0):
                        dve.wait_ge(shift_placed[g], 16 * PARTS * (bb + 1))
                    k = PARTS * GROUP * QTILES
                    dve.tensor_copy(negT[r % 2][:, :], bank.bitcast(BF16)[0:k, 0:P]).then_inc(item_taken, 1)
                elif it[0] == "o":
                    t = it[1]
                    o = bank.rearrange("p (h w) -> p h w", w=32)
                    dve.reciprocal(rden[:, t, :], o[:, :, HD]).then_inc(rden_ready, 1)
                    dve.wait_ge(rden_ready, QTILES * b + t + 1)
                    dve.tensor_tensor(o_norm[:, t, :, :], o[:, :, 0:HD],
                                      rden[:, t, :].unsqueeze(2).to_broadcast([P, HEADS, HD]), ALU.mult
                                      ).then_inc(item_taken, 1)
                elif it[0] == "n":
                    dve.tensor_copy(o_normT[:, 2 * it[1]:2 * it[1] + 2, :, :].rearrange("p t h q -> p (t h q)"),
                                    bank).then_inc(item_taken, 1)
                else:
                    t = it[1]
                    dve.wait_ge(resid_ready, QTILES * b + t + 1)
                    dve.tensor_tensor(y[:, t, :], bank[:, 0:DIM], resid[:, t, :], ALU.add
                                      ).then_inc(item_taken, 1)
                    dve.wait_ge(item_taken, at + 1)
                    dve.bn_stats(stats[:, t, :], y[:, t, :]).then_inc(stats_ready, 1)

            def shift(b, r, step):
                n = r % 2
                if step:
                    dve.wait_ge(shift_step, SHIFT_STEPS * (GROUPS * b + r) + step)
                else:
                    dve.wait_ge(item_taken, LOOP_ITEMS * b + last_max[r] + 1)
                if step == 0:
                    made = dve.tensor_reduce(neg[n][:, :], mx[n][:, :, :, :].rearrange("p h t c -> p (h t) c"), AX.X,
                                             ALU.max, negate=True)
                elif step == 1:
                    made = dve.tensor_copy(negparts[n][:, 0, :], neg[n][:, :])
                elif step == 2:
                    made = dve.tensor_tensor(negleft[n][:, :], neg[n][:, :], negparts[n][:, 0, :], ALU.subtract)
                elif step == 3:
                    made = dve.tensor_copy(negparts[n][:, 1, :], negleft[n][:, :])
                else:
                    made = dve.tensor_tensor(negparts[n][:, 2, :], negleft[n][:, :], negparts[n][:, 1, :],
                                             ALU.subtract)
                made.then_inc(shift_step, 1)

            def statistics(b, t):
                dve.bn_aggr(mv[:, t, :], stats[:, t, :]).then_inc(mv_ready, 1)

            def normalise(b, t):
                dve.wait_ge(norm_step, NORM_STEPS * QTILES * b + 2 * t + 2)
                dve.tensor_scalar(z[:, t, :], y[:, t, :], mv[:, t, 0:1], rstd[:, t, 1:2],
                                  ALU.subtract, ALU.mult).then_inc(z_ready, 1)

            def scale_last():
                for t in range(QTILES):
                    dve.wait_ge(z_ready, QTILES * (BATCHES - 1) + t + 1)
                    dve.tensor_tensor(z[:, t, :], z[:, t, :], g_row[:, :], ALU.mult).then_inc(last_scaled, 1)
                for t in range(QTILES):
                    dve.wait_ge(last_scaled, t + 1)
                    dve.tensor_tensor(z[:, t, :], z[:, t, :], b_row[:, :], ALU.add).then_inc(last_ready, 1)

            def items(b, slots):
                flat = [x for slot in slots for x in slot]

                def kind_at(at):
                    return flat[at][1] if 0 <= at < len(flat) else ("none",)

                def shift_steps(at):
                    return [(kind_at(at - 1 - step)[1], step) for step in range(SHIFT_STEPS)
                            if is_last_maxima(kind_at(at - 1 - step))
                            and not any(kind_at(i)[0] == "m" for i in range(at - step, at + 1))]

                for at in range(len(flat) + max(NORM_LAG, SHIFT_STEPS)):
                    it = kind_at(at)
                    if it[0] == "m":
                        for step in range(SHIFT_STEPS):
                            if any(is_last_maxima(kind_at(i)) for i in range(at - 1 - step, at)):
                                shift(b, it[1], step)
                    if kind_at(at - 1)[0] == "y":
                        dve.wait_ge(stats_ready, QTILES * b + kind_at(at - 1)[1] + 1)
                    if at < len(flat):
                        item(b, flat[at][0], it)
                    if is_last_maxima(it):
                        last_max[it[1]] = flat[at][0]
                    if kind_at(at - NORM_LAG)[0] == "y":
                        normalise(b, kind_at(at - NORM_LAG)[1])
                    if kind_at(at - 1)[0] == "y":
                        statistics(b, kind_at(at - 1)[1])
                    for r, step in shift_steps(at):
                        shift(b, r, step)

            last_max = {}
            items(0, [plan.prologue] + plan.unit0)
            with dve.Fori(0, BATCHES - 1) as b:
                items(b, [slot for slots in plan.body for slot in slots])
            items(BATCHES - 1, [slot for slots in plan.tail for slot in slots])
            items(BATCHES - 1, [plan.ending])
            scale_last()

        @block.tensor
        def _(pe):
            pe.wait_ge(ident_made, 1)

            def bank_free(b, n):
                before = n - BANKS
                if before >= 0:
                    pb = b
                else:
                    before = n + (NPIECES - 1 - n) // BANKS * BANKS
                    pb = b - 1
                count = sum(BY_DVE[i] == BY_DVE[before] for i in range(before + 1))
                if isinstance(pb, int) and pb < 0:
                    return
                if before < TURNS:
                    pe.wait_ge(lo_took, TURNS * pb + before + 1)
                elif BY_DVE[before]:
                    pe.wait_ge(dve_took, DVE_PIECES * pb + count)
                else:
                    pe.wait_ge(act_took, ACT_PIECES * pb + count)

            products = [(k, pair) for k in range(HALVES) for pair in PAIRS]

            def early_score(b, n, chunk, tiles):
                h, i = divmod(n, EARLY_TILES)
                if n < 2:
                    bank_free(b, NPIECES - 2 + n)
                    pe.wait_ge(kq_loaded[0], 16 * KQ_DMAS)
                else:
                    pe.wait_ge(item_taken, EARLY * (2 * chunk + tiles) + n - 1)
                pe.matmul(psum[:, early_bank(n), :],
                          qrys[0][0:PROD, h, bass.ds((EARLY_TILES * tiles + i) * P, P)],
                          keys[0][0:PROD, h, bass.ds(chunk * BANK, BANK)], start=True, stop=True
                          ).then_inc(item_made, 1)

            def project(b, early=None):
                for n, (kind, h, c) in enumerate(PIECES):
                    bank, (first, width) = psum[:, n % BANKS, :], columns(kind, c)
                    if early:
                        for e in EARLY_AT[n]:
                            early_score(b, e, *early)
                    if early and n >= NPIECES - 2:
                        pe.wait_ge(item_taken, EARLY * (2 * early[0] + early[1] + 1) - (NPIECES - 1 - n))
                    else:
                        bank_free(b, n)
                    if n == 0:
                        pe.wait_ge(x_loaded, 16 * (b + 1))
                    if kind == "ct" and h == 0 and c != 1:
                        pe.wait_ge(ctx_loaded[max(c - 1, 0)], 16 * (b + 1))
                    if n == TURNS:
                        pe.wait_ge(lo_took, TURNS * b + HALVES)
                        if is_first(b):
                            pe.wait_ge(weights_lo, 1)
                            pe.wait_ge(consts_made, CONSTS)
                    if kind == "v":
                        chunk = min(h + 1, KTILES - 1) // QTILES
                        pe.wait_ge(lo_took, TURNS * b + HALVES * (chunk + 2))
                    if kind == "xt":
                        for t in range(QTILES):
                            mm = pe.transpose(bank[:, t * P:(t + 1) * P], x_in[:, t, h * P:(h + 1) * P], ident[:, :])
                    elif kind == "ct":
                        for i in range(0, width, P):
                            w = min(P, width - i)
                            mm = pe.transpose(bank[:, i:i + w], ctx_in[0:w, (c * BANK + i) // P, h * P:(h + 1) * P],
                                              ident[0:w, 0:w])
                    elif kind == "v":
                        for i in range(min(2, KTILES - h)):
                            w = P if h + i < FULL else REST
                            for n_mm, (k, (pc, pw)) in enumerate(products):
                                mm = pe.matmul(bank[0:w, i * DIM:(i + 1) * DIM],
                                               ctxT[pc][:, k, (h + i) * P:(h + i) * P + w], wparts[pw][:, 2, k, :],
                                               start=(n_mm == 0), stop=(n_mm == len(products) - 1))
                    else:
                        w, src = (1, ctxT) if kind == "k" else (0, xT)
                        even = width + width % 2
                        for n_mm, (k, (pw, px)) in enumerate(products):
                            mm = pe.matmul(bank[:, 0:even], wparts[pw][:, w, k, h * P:(h + 1) * P],
                                           src[px][:, k, first:first + even],
                                           start=(n_mm == 0), stop=(n_mm == len(products) - 1))
                    mm.then_inc(piece_made, 1)

            for b in range(EARLY_FROM):
                project(b)
            with pe.Fori(0, EARLY_CHUNKS) as chunk:
                with pe.Fori(0, 2) as tiles:
                    project(EARLY_FROM + 2 * chunk + tiles, (chunk, tiles))
            pe.wait_ge(act_took, ACT_PIECES * BATCHES)
            pe.wait_ge(dve_took, DVE_PIECES * BATCHES)
            pe.wait_ge(wo_loaded, 16)
            pe.matmul(o_bank, zeros[0:PROD, 0:P], zeros[0:PROD, :], start=True, stop=True)

            def item(b, n, it):
                at = LOOP_ITEMS * b + n
                bank = ring[n % RING]
                pe.wait_ge(item_taken, at - RING + 1)
                if it[0] == "s":
                    _, r, h, j = it
                    bb, g = vitem(b, r)
                    if h == 0 and j == 0:
                        pe.wait_ge(kq_loaded[g], 16 * KQ_DMAS * (bb + 1))
                    if j < SMAX - 1:
                        t, c = divmod(j, len(CHUNKS) - 1)
                        mm = pe.matmul(bank, qrys[g][0:PROD, h, t * P:(t + 1) * P],
                                       keys[g][0:PROD, h, c * BANK:(c + 1) * BANK], start=True, stop=True)
                    else:
                        for t in range(QTILES):
                            mm = pe.matmul(bank[:, t * REST:(t + 1) * REST], qrys[g][0:PROD, h, t * P:(t + 1) * P],
                                           keys[g][0:PROD, h, KEYS - REST:KEYS], start=True, stop=True)
                elif it[0] == "m":
                    r = it[1]
                    pe.wait_ge(shift_step, SHIFT_STEPS * (GROUPS * b + r + 1))
                    mm = pe.transpose(bank.bitcast(BF16)[:, 0:P], negpad[r % 2][:, :], identb[:, :])
                elif it[0] == "o":
                    t = it[1]
                    pe.wait_ge(o_copied, GROUPS * (b + 1))
                    for g in range(GROUPS):
                        mm = pe.transpose(bank[:, g * P:(g + 1) * P], o_out[:, g, t * P:(t + 1) * P], ident[:, :])
                elif it[0] == "n":
                    pe.wait_ge(item_taken, LOOP_ITEMS * b + ending_at[("o", 2 * it[1] + 1)] + 1)
                    for i in range(2):
                        src = o_norm[:, 2 * it[1] + i, :, :].rearrange("p h d -> p (h d)")
                        for h in range(HALVES):
                            mm = pe.transpose(bank[:, (i * HALVES + h) * P:(i * HALVES + h + 1) * P],
                                              src[:, h * P:(h + 1) * P], ident[:, :])
                else:
                    t = it[1]
                    pe.wait_ge(item_taken, LOOP_ITEMS * b + ending_at[("n", t // 2)] + 1)
                    for h in range(HALVES):
                        mm = pe.matmul(bank[:, 0:DIM], o_normT[:, t, h, :], wo[:, h, :],
                                       start=(h == 0), stop=(h == HALVES - 1))
                mm.then_inc(item_made, 1)

            def scores(b, r, kt, h):
                p, i = divmod(h, 2)
                u = GROUPS * b + r
                s = KTILES * u + kt
                bb, g = vitem(b, r)
                if i == 0 and not (isinstance(u, int) and s == 0):
                    pe.wait_ge(probs_ready, 2 * s + p - 1)
                if kt == 0 and h == 0:
                    pe.wait_ge(ones_made, g + 1)
                    pe.wait_ge(shift_placed[g], 16 * PARTS * (bb + 1))
                w = P if kt < FULL else REST
                mm = pe.matmul(s_bank[p][i][0:w, :], keys[g][:, 2 * p + i, kt * P:kt * P + w],
                               qrys[g][:, 2 * p + i, :], start=True, stop=True)
                if i == 1:
                    mm.then_inc(scores_ready, 1)

            def times_v(b, r, kt):
                u = GROUPS * b + r
                s = KTILES * u + kt
                bb, g = vitem(b, r)
                pe.wait_ge(probs_ready, 2 * s + 2)
                if kt == 0:
                    pe.wait_ge(v_loaded[g], 16 * V_DMAS * (bb + 1))
                    pe.wait_ge(o_copied, u)
                w = P if kt < FULL else REST
                buf = (KTILES * r + kt) % PBUFS
                for h in range(GROUP):
                    mm = pe.matmul(o_bank[32 * h:32 * h + VW, :], vals[g][0:w, kt, h, :],
                                   probs[0:w, buf, h * BANK:(h + 1) * BANK],
                                   start=(kt == 0), stop=(kt == KTILES - 1))
                mm.then_inc(pv_done, 1)

            def unit(b, r, slots, first=False):
                for kt in range(KTILES):
                    for h in range(GROUP):
                        scores(b, r, kt, h)
                        for n, it in slots[GROUP * kt + h]:
                            item(b, n, it)
                    if kt:
                        times_v(b, r, kt - 1)
                    elif not first:
                        times_v(b, r - 1, KTILES - 1)

            ending_at = {it: n for slots in plan.body for slot in slots for n, it in slot}
            for n, it in plan.prologue:
                item(0, n, it)
            unit(0, 0, plan.unit0, first=True)
            with pe.Fori(0, BATCHES - 1) as b:
                for r in range(1, GROUPS + 1):
                    unit(b, r, plan.body[r - 1])
            for r in range(1, GROUPS):
                unit(BATCHES - 1, r, plan.tail[r - 1])
            times_v(BATCHES - 1, GROUPS - 1, KTILES - 1)
            ending_at = {it: n for n, it in plan.ending}
            for n, it in plan.ending:
                item(BATCHES - 1, n, it)


_INS = ["x", "ctx_1024", "L0_xattn_Wq", "L0_xattn_bq", "L0_xattn_Wk", "L0_xattn_bk", "L0_xattn_Wv", "L0_xattn_bv",
        "L0_xattn_Wo", "L0_xattn_bo", "L0_xattn_ln_g", "L0_xattn_ln_b"]


def kernel(**inputs):
    import numpy as np
    import concourse.bacc as bacc
    from concourse.bass_utils import run_bass_kernel_spmd

    nc = bacc.Bacc("TRN2", target_bir_lowering=False, num_devices=1)
    arrays, args = {}, []
    for name in _INS:
        a = np.ascontiguousarray(inputs[name])
        arrays[f"in_{name}"] = a
        args.append(nc.dram_tensor(f"in_{name}", a.shape, mybir.dt.from_np(a.dtype), kind="ExternalInput").ap())
    out = nc.dram_tensor("out_x", (BATCHES, QUERIES, DIM), F32, kind="ExternalOutput").ap()
    xattn_kernel(nc, *args, out)
    r = run_bass_kernel_spmd(nc, [arrays], core_ids=[0])
    return r.results[0]["out_x"]
```
